# Optimizing a Trainium2 kernel written in Bass

```python
import numpy as np
import jax
import jax.numpy as jnp

def _softmax(x, axis=-1):
    return jax.nn.softmax(x, axis=axis)

def _gelu(x):
    return jax.nn.gelu(x, approximate=True)

def _silu(x):
    return jax.nn.silu(x)

def _sigmoid(x):
    return jax.nn.sigmoid(x)

def _layernorm(x, axis=-1, eps=1e-05):
    m = jnp.mean(x, axis=axis, keepdims=True)
    v = jnp.var(x, axis=axis, keepdims=True)
    return (x - m) / jnp.sqrt(v + eps)

def _scatter_add(tgt, idx, src, axis=0):
    return tgt.at[idx].add(src)

def _segment_sum(src, seg, n):
    return jax.ops.segment_sum(src, seg, n)
kernel_name = 'mk_vit_tower_postln_d1_tok_img256_r4_0890c2'

def setup_inputs(seed: int=0):
    np.random.seed(seed)
    _w = jnp.asarray

    def _rec_inputs():
        import jax
        import jax.numpy as jnp
        _rk = jax.random.key(seed)
        x = -0.000125008 + 0.999885 * jax.random.normal(jax.random.fold_in(_rk, 1), (128, 64, 64, 64), jnp.float32)
        return x
    x = _rec_inputs()

    def _L0_tok_setup():
        import jax, jax.numpy as jnp
        import numpy as np
        B, C, H, W = (32, 64, 64, 64)
        STRIDE, HEADS = (4, 8)

        def _ln(x, w, b):
            mu = x.mean(-1, keepdims=True)
            var = ((x - mu) ** 2).mean(-1, keepdims=True)
            return (x - mu) * jax.lax.rsqrt(var + 1e-05) * w + b
        key = jax.random.key(seed)
        ks = jax.random.split(key, 4)
        return {'features': jax.random.normal(ks[0], (B, C, H, W), dtype=jnp.float32), 'ln_q_w': jnp.ones((C,), jnp.float32), 'ln_q_b': jnp.zeros((C,), jnp.float32), 'Wq': jax.random.normal(ks[1], (C, C), dtype=jnp.float32) * 0.02, 'ln_kv_w': jnp.ones((C,), jnp.float32), 'ln_kv_b': jnp.zeros((C,), jnp.float32), 'Wkv': jax.random.normal(ks[2], (2 * C, C), dtype=jnp.float32) * 0.02, 'proj_w': jax.random.normal(ks[3], (C, C), dtype=jnp.float32) * 0.02, 'proj_b': jnp.zeros((C,), jnp.float32), 'conv_stride': STRIDE, 'num_heads': HEADS}
    _L0_tok_all = _L0_tok_setup()
    _L0_tok_in = {k: v for k, v in _L0_tok_all.items() if k in ('ln_q_w', 'ln_q_b', 'Wq', 'ln_kv_w', 'ln_kv_b', 'Wkv', 'proj_w', 'proj_b')}
    del _L0_tok_all

    def _L0_attn_setup():
        import jax, jax.numpy as jnp
        import numpy as np
        import math
        CHUNK = 128

        def _build_slopes(n):

            def p2(n):
                start = 2.0 ** (-2.0 ** (-(math.log2(n) - 3)))
                return [start ** (i + 1) for i in range(n)]
            if math.log2(n).is_integer():
                s = p2(n)
            else:
                c = 2 ** math.floor(math.log2(n))
                s = p2(c) + p2(2 * c)[0::2][:n - c]
            return np.asarray(s, dtype=np.float32)

        def _lightning_attn(q, k, v, slopes):
            b, h, l, d = q.shape
            n = l // CHUNK
            s = slopes.reshape(h, 1, 1)
            pos = jnp.arange(CHUNK, dtype=q.dtype)
            diff = pos[:, None] - pos[None, :]
            mask = jnp.where(diff >= 0, jnp.exp(-s * diff), 0.0)[None]
            q_dec = jnp.exp(-slopes[:, None] * pos)[None, :, :, None]
            k_dec = jnp.exp(-slopes[:, None] * (CHUNK - pos))[None, :, :, None]
            blk = jnp.exp(-slopes * CHUNK).reshape(1, h, 1, 1)
            qc = q.reshape(b, h, n, CHUNK, d).transpose(2, 0, 1, 3, 4)
            kc = k.reshape(b, h, n, CHUNK, d).transpose(2, 0, 1, 3, 4)
            vc = v.reshape(b, h, n, CHUNK, d).transpose(2, 0, 1, 3, 4)

            def step(S, xs):
                qi, ki, vi = xs
                scores = jnp.einsum('bhcd,bhed->bhce', qi, ki) * mask
                intra = jnp.einsum('bhce,bhed->bhcd', scores, vi)
                inter = jnp.einsum('bhcd,bhde->bhce', qi * q_dec, S)
                S_new = blk * S + jnp.einsum('bhcd,bhce->bhde', ki * k_dec, vi)
                return (S_new, intra + inter)
            S0 = jnp.zeros((b, h, d, d), q.dtype)
            _, o = jax.lax.scan(step, S0, (qc, kc, vc))
            return o.transpose(1, 2, 0, 3, 4).reshape(b, h, l, d)
        key = jax.random.key(seed)
        k1, k2, k3 = jax.random.split(key, 3)
        b, l, c, h = (8, 4096, 64, 8)
        x = jax.random.normal(k1, (b, l, c), dtype=jnp.float32)
        w_qkv = jax.random.normal(k2, (c, 3 * c), dtype=jnp.float32) * 0.02
        w_proj = jax.random.normal(k3, (c, c), dtype=jnp.float32) * 0.02
        b_proj = jnp.zeros((c,), dtype=jnp.float32)
        slopes = jnp.asarray(_build_slopes(h))
        return {'x': x, 'w_qkv': w_qkv, 'w_proj': w_proj, 'b_proj': b_proj, 'slopes': slopes}
    _L0_attn_all = _L0_attn_setup()
    _L0_attn_in = {k: v for k, v in _L0_attn_all.items() if k in ('w_qkv', 'w_proj', 'b_proj', 'slopes')}
    del _L0_attn_all

    def _L0_ffn_setup():
        import jax, jax.numpy as jnp
        import numpy as np
        NUM_EXPERTS = 8
        TOP_K = 2
        B, S, D = (8, 2048, 64)

        def _moe(tokens, router_w, w1, b1, w2, b2):
            N = tokens.shape[0]
            E = router_w.shape[0]
            logits = tokens.astype(jnp.float32) @ router_w.astype(jnp.float32).T
            probs = jax.nn.softmax(logits, axis=-1)
            rw, re = jax.lax.top_k(probs, TOP_K)
            if TOP_K > 1:
                rw = rw / jnp.maximum(rw.sum(-1, keepdims=True), 1e-12)
            rw = rw.astype(tokens.dtype)
            combine = jnp.zeros((N, E), tokens.dtype).at[jnp.arange(N)[:, None], re].set(rw)
            out = tokens
            for e in range(E):
                h = jax.nn.gelu(tokens @ w1[e] + b1[e], approximate=False)
                y = h @ w2[e] + b2[e]
                out = out + combine[:, e:e + 1] * y
            return out
        key = jax.random.key(seed)
        ks = jax.random.split(key, 4)
        scale = 1.0 / np.sqrt(D).astype(np.float32)
        return {'input_embeddings': jax.random.normal(ks[0], (B, S, D), jnp.float32), 'router_w': jax.random.normal(ks[1], (NUM_EXPERTS, D), jnp.float32) * scale, 'w1': jax.random.normal(ks[2], (NUM_EXPERTS, D, D), jnp.float32) * scale, 'b1': jnp.zeros((NUM_EXPERTS, D), jnp.float32), 'w2': jax.random.normal(ks[3], (NUM_EXPERTS, D, D), jnp.float32) * scale, 'b2': jnp.zeros((NUM_EXPERTS, D), jnp.float32)}
    _L0_ffn_all = _L0_ffn_setup()
    _L0_ffn_in = {k: v for k, v in _L0_ffn_all.items() if k in ('router_w', 'w1', 'b1', 'w2', 'b2')}
    del _L0_ffn_all
    return {'x': x, 'L0_tok_ln_q_w': _L0_tok_in['ln_q_w'], 'L0_tok_ln_q_b': _L0_tok_in['ln_q_b'], 'L0_tok_Wq': _L0_tok_in['Wq'], 'L0_tok_ln_kv_w': _L0_tok_in['ln_kv_w'], 'L0_tok_ln_kv_b': _L0_tok_in['ln_kv_b'], 'L0_tok_Wkv': _L0_tok_in['Wkv'], 'L0_tok_proj_w': _L0_tok_in['proj_w'], 'L0_tok_proj_b': _L0_tok_in['proj_b'], 'L0_attn_w_qkv': _L0_attn_in['w_qkv'], 'L0_attn_w_proj': _L0_attn_in['w_proj'], 'L0_attn_b_proj': _L0_attn_in['b_proj'], 'L0_attn_slopes': _L0_attn_in['slopes'], 'L0_ffn_router_w': _L0_ffn_in['router_w'], 'L0_ffn_w1': _L0_ffn_in['w1'], 'L0_ffn_b1': _L0_ffn_in['b1'], 'L0_ffn_w2': _L0_ffn_in['w2'], 'L0_ffn_b2': _L0_ffn_in['b2']}

def reference(x, L0_tok_ln_q_w, L0_tok_ln_q_b, L0_tok_Wq, L0_tok_ln_kv_w, L0_tok_ln_kv_b, L0_tok_Wkv, L0_tok_proj_w, L0_tok_proj_b, L0_attn_w_qkv, L0_attn_w_proj, L0_attn_b_proj, L0_attn_slopes, L0_ffn_router_w, L0_ffn_w1, L0_ffn_b1, L0_ffn_w2, L0_ffn_b2):
    import jax
    import jax.numpy as jnp

    def _L0_tok_ref(features, ln_q_w, ln_q_b, Wq, ln_kv_w, ln_kv_b, Wkv, proj_w, proj_b, conv_stride, num_heads):
        import jax, jax.numpy as jnp
        import numpy as np
        B, C, H, W = (32, 64, 64, 64)
        STRIDE, HEADS = (4, 8)

        def _ln(x, w, b):
            mu = x.mean(-1, keepdims=True)
            var = ((x - mu) ** 2).mean(-1, keepdims=True)
            return (x - mu) * jax.lax.rsqrt(var + 1e-05) * w + b
        s = conv_stride
        b, c, hh, ww = features.shape
        h, w = (hh // s, ww // s)
        hw, n, d = (h * w, s * s, c // num_heads)
        scale = c ** (-0.5)
        x = features.reshape(b, c, h, s, w, s)
        reduce_feats = x.mean((3, 5)).reshape(b, c, hw).transpose(0, 2, 1)
        unf = x.transpose(0, 1, 2, 4, 3, 5).reshape(b, c, hw, n).transpose(0, 2, 3, 1)
        q = _ln(reduce_feats, ln_q_w, ln_q_b) @ Wq.T
        q = q.reshape(b, hw, num_heads, d).transpose(0, 2, 1, 3)
        kv = _ln(unf, ln_kv_w, ln_kv_b) @ Wkv.T
        kv = kv.reshape(b, hw, n, 2, num_heads, d).transpose(3, 0, 4, 1, 2, 5)
        k, v = (kv[0], kv[1])
        attn = jax.nn.softmax(jnp.einsum('bhpd,bhpnd->bhpn', q * scale, k), axis=-1)
        aggre = jnp.einsum('bhpn,bhpnd->bhpd', attn, v)
        aggre = aggre.transpose(0, 2, 1, 3).reshape(b, hw, c)
        return reduce_feats + aggre @ proj_w.T + proj_b

    def _L0_attn_ref(x, w_qkv, w_proj, b_proj, slopes):
        import jax, jax.numpy as jnp
        import numpy as np
        import math
        CHUNK = 128

        def _build_slopes(n):

            def p2(n):
                start = 2.0 ** (-2.0 ** (-(math.log2(n) - 3)))
                return [start ** (i + 1) for i in range(n)]
            if math.log2(n).is_integer():
                s = p2(n)
            else:
                c = 2 ** math.floor(math.log2(n))
                s = p2(c) + p2(2 * c)[0::2][:n - c]
            return np.asarray(s, dtype=np.float32)

        def _lightning_attn(q, k, v, slopes):
            b, h, l, d = q.shape
            n = l // CHUNK
            s = slopes.reshape(h, 1, 1)
            pos = jnp.arange(CHUNK, dtype=q.dtype)
            diff = pos[:, None] - pos[None, :]
            mask = jnp.where(diff >= 0, jnp.exp(-s * diff), 0.0)[None]
            q_dec = jnp.exp(-slopes[:, None] * pos)[None, :, :, None]
            k_dec = jnp.exp(-slopes[:, None] * (CHUNK - pos))[None, :, :, None]
            blk = jnp.exp(-slopes * CHUNK).reshape(1, h, 1, 1)
            qc = q.reshape(b, h, n, CHUNK, d).transpose(2, 0, 1, 3, 4)
            kc = k.reshape(b, h, n, CHUNK, d).transpose(2, 0, 1, 3, 4)
            vc = v.reshape(b, h, n, CHUNK, d).transpose(2, 0, 1, 3, 4)

            def step(S, xs):
                qi, ki, vi = xs
                scores = jnp.einsum('bhcd,bhed->bhce', qi, ki) * mask
                intra = jnp.einsum('bhce,bhed->bhcd', scores, vi)
                inter = jnp.einsum('bhcd,bhde->bhce', qi * q_dec, S)
                S_new = blk * S + jnp.einsum('bhcd,bhce->bhde', ki * k_dec, vi)
                return (S_new, intra + inter)
            S0 = jnp.zeros((b, h, d, d), q.dtype)
            _, o = jax.lax.scan(step, S0, (qc, kc, vc))
            return o.transpose(1, 2, 0, 3, 4).reshape(b, h, l, d)
        b, l, c = x.shape
        h = slopes.shape[0]
        d = c // h
        scale = d ** (-0.5)
        qkv = (x @ w_qkv).reshape(b, l, 3, h, d)
        q = qkv[:, :, 0].transpose(0, 2, 1, 3) * scale
        k = qkv[:, :, 1].transpose(0, 2, 1, 3)
        v = qkv[:, :, 2].transpose(0, 2, 1, 3)
        o = _lightning_attn(q, k, v, slopes)
        out = o.transpose(0, 2, 1, 3).reshape(b, l, c) @ w_proj + b_proj
        return out

    def _L0_ffn_ref(input_embeddings, router_w, w1, b1, w2, b2):
        import jax, jax.numpy as jnp
        import numpy as np
        NUM_EXPERTS = 8
        TOP_K = 2
        B, S, D = (8, 2048, 64)

        def _moe(tokens, router_w, w1, b1, w2, b2):
            N = tokens.shape[0]
            E = router_w.shape[0]
            logits = tokens.astype(jnp.float32) @ router_w.astype(jnp.float32).T
            probs = jax.nn.softmax(logits, axis=-1)
            rw, re = jax.lax.top_k(probs, TOP_K)
            if TOP_K > 1:
                rw = rw / jnp.maximum(rw.sum(-1, keepdims=True), 1e-12)
            rw = rw.astype(tokens.dtype)
            combine = jnp.zeros((N, E), tokens.dtype).at[jnp.arange(N)[:, None], re].set(rw)
            out = tokens
            for e in range(E):
                h = jax.nn.gelu(tokens @ w1[e] + b1[e], approximate=False)
                y = h @ w2[e] + b2[e]
                out = out + combine[:, e:e + 1] * y
            return out
        b, s, d = input_embeddings.shape
        tokens = input_embeddings.reshape(b * s, d)
        return _moe(tokens, router_w, w1, b1, w2, b2).reshape(b, s, d)
    h = _L0_tok_ref(x, L0_tok_ln_q_w, L0_tok_ln_q_b, L0_tok_Wq, L0_tok_ln_kv_w, L0_tok_ln_kv_b, L0_tok_Wkv, L0_tok_proj_w, L0_tok_proj_b, 4, 8)
    h = _layernorm(h + _L0_attn_ref(h, L0_attn_w_qkv, L0_attn_w_proj, L0_attn_b_proj, L0_attn_slopes), axis=-1)
    h = _layernorm(h + _L0_ffn_ref(h, L0_ffn_router_w, L0_ffn_w1, L0_ffn_b1, L0_ffn_w2, L0_ffn_b2), axis=-1)
    return h

_drawn_inputs = setup_inputs


def setup_inputs(seed=0):
    import zlib

    import numpy as np

    out = dict(_drawn_inputs(seed))
    spreads = {'L0_tok_ln_q_w': (1.0, 0.6),
     'L0_tok_ln_q_b': (0.0, 2.0),
     'L0_tok_ln_kv_w': (1.0, 0.6),
     'L0_tok_ln_kv_b': (0.0, 0.395),
     'L0_tok_proj_b': (0.0, 0.1),
     'L0_attn_b_proj': (0.0, 0.1),
     'L0_ffn_b1': (0.0, 0.345),
     'L0_ffn_b2': (0.0, 0.1)}
    factors = {'L0_tok_Wq': 26.121, 'L0_attn_w_qkv': 8.0, 'L0_attn_w_proj': 8.0, 'L0_attn_slopes': 8.0}
    for name, (base, spread) in spreads.items():
        noise = np.random.default_rng([zlib.crc32(name.encode()), seed]).standard_normal(out[name].shape)
        drawn = base * np.exp(spread * noise) if base else spread * noise
        out[name] = jnp.asarray(drawn.astype(out[name].dtype))
    for name, factor in factors.items():
        out[name] = (out[name] * factor).astype(out[name].dtype)
    return out
```

```python
from contextlib import ExitStack

import concourse.bass as bass
from concourse import mybir

ALU = mybir.AluOpType
ACT = mybir.ActivationFunctionType
AX = mybir.AxisListType.X
F32 = mybir.dt.float32
I32 = mybir.dt.int32


def vit_tower_kernel(nc, x, ln_q_w, ln_q_b, Wq, ln_kv_w, ln_kv_b, Wkv, proj_w, proj_b,
                     w_qkv, w_proj, b_proj, slopes, router_w, w1, b1, w2, b2, out):
    P = 128
    B, C, HH, WW = x.shape
    ST = 4
    N = ST * ST
    PX = HH * WW // 2
    HEADS = slopes.shape[0]
    D = C // HEADS
    E = router_w.shape[0]
    SL = 2 * HEADS
    UNITS = B
    TOK_SCALE = float(C) ** -0.5
    ATT_SCALE = float(D) ** -0.5
    EPS = 1e-5
    GN = 4
    NG = N // GN
    assert (C, D, N, P) == (64, 8, 16, 128) and B % 2 == 0

    def done(i, s, lag, per):
        if isinstance(i, int):
            return max(0, min(UNITS, 2 * i + s - lag + 1)) * per
        return i * (2 * per) + (s - lag + 1) * per

    def there(i, s, lag):
        return not isinstance(i, int) or 0 <= 2 * i + s - lag < UNITS

    def pairs_done(i, back):
        if isinstance(i, int):
            return max(0, min(UNITS // 2, i + back))
        return i + back

    def floor0(n):
        return max(0, n) if isinstance(n, int) else n

    def chain(eng, sem, base):
        n = [0]

        def link(ins):
            n[0] += 1
            ins.then_inc(sem, 1)
            eng.wait_ge(sem, floor0(base + n[0]))
        return link, n

    def units(eng, step):
        step(-1, 1)
        for i in (0, 1, 2):
            step(i, 0)
            step(i, 1)
        with eng.Fori(3, UNITS // 2 - 1) as i:
            step(i, 0)
            step(i, 1)
        for i in (UNITS // 2 - 1, UNITS // 2, UNITS // 2 + 1):
            step(i, 0)
            step(i, 1)

    with ExitStack() as ctx:
        def sb(name, shape, dt=F32):
            return ctx.enter_context(nc.sbuf_tensor(name, shape, dt))

        def sem(name):
            return ctx.enter_context(nc.semaphore(name))

        ps = ctx.enter_context(nc.psum_tensor("ps", [P, 8, 512], F32))
        psf = ps[:].rearrange("p b c -> p (b c)")
        CV = [psf[:, 0:1024], psf[:, 1024:2048]]
        KB = [ps[:, 4, :], ps[:, 5, :]]
        B6, B7 = ps[:, 6, :], ps[:, 7, :]
        SCB = [ps[:, 4, :], ps[:, 5, :], ps[:, 0, :], ps[:, 1, :]]
        QKB, VKB = ps[:, 2, :], ps[:, 3, :]

        ident = sb("ident", [P, P])
        ident2 = sb("ident2", [P, P])
        ones = sb("ones", [P, P])
        blockmask = sb("blockmask", [P, P])
        headmask = sb("headmask", [P, SL])
        w_ckv = sb("w_ckv", [P, 3 * P])
        w_q_id = sb("w_q_id", [P, 2 * P])
        w_pj = sb("w_pj", [P, P])
        w_aq = sb("w_aq", [P, P])
        w_avki = sb("w_avki", [P, 3 * P])
        w_ap = sb("w_ap", [P, P])
        bk_row = sb("bk_row", [P, P])
        bq_row = sb("bq_row", [P, P])
        bp_row = sb("bp_row", [P, P])
        bv_col = sb("bv_col", [P, 1])
        pb_col = sb("pb_col", [P, 1])
        decay = sb("decay", [P, HEADS, P])
        kdec = sb("kdec", [P, HEADS])
        qdec = sb("qdec", [P, P])
        h1 = sb("h1", [P, UNITS, P])
        eps_col = sb("eps_col", [P, 1])

        with ExitStack() as early:
            def sb1(name, shape, dt=F32):
                return early.enter_context(nc.sbuf_tensor(name, shape, dt))

            rows = sb1("rows", [P, 4, 64])
            lnb = sb1("lnb", [P, 4, 64])
            cat = sb1("cat", [P, 4, P])
            scr = sb1("scr", [P, 4, P])
            col = sb1("col", [P, 8])
            diff = sb1("diff", [P, P])
            diffi = sb1("diffi", [P, P], I32)
            posi = sb1("posi", [P, 1], I32)
            pos = sb1("pos", [P, 3])
            slb = sb1("slb", [P, 8])
            nsl = sb1("nsl", [P, 8])
            qd_tok = sb1("qd_tok", [P, P])
            bprow64 = sb1("bprow64", [P, 64])
            tril = sb1("tril", [P, P])
            xb = sb1("xb", [P, 2, PX])
            sq = sb1("sq", [P, 2, N * P])
            vs = sb1("vs", [P, 2, N * P])
            kq = sb1("kq", [P, N * P])
            pv = sb1("pv", [P, N * P])
            ssq = sb1("ssq", [P, 2, 2 * N])
            var = sb1("var", [P, 2 * N])
            yrs = sb1("yrs", [P, 2 * N])
            yt = sb1("yt", [P, 2 * N])
            sc = sb1("sc", [P, N * SL])
            ex = sb1("ex", [P, N * SL])
            aw = sb1("aw", [P, N * SL])
            mx = sb1("mx", [P, SL])
            den = sb1("den", [P, SL])
            rden = sb1("rden", [P, SL])
            agg = sb1("agg", [P, P])
            aggn = sb1("aggn", [P, P])
            aggT = sb1("aggT", [P, P])
            rsum = sb1("rsum", [P, P])
            red = sb1("red", [P, 2, P])
            hT = sb1("hT", [P, 2, P])
            qc = sb1("qc", [P, P])
            q2 = sb1("q2", [P, P])
            qq = sb1("qq", [P, P])
            qst = sb1("qst", [P, 8, 2])
            sbias = sb1("sbias", [P, SL])
            qT = sb1("qT", [P, 2, P])
            kT = sb1("kT", [P, 2, P])
            VW = P + D
            vpad = sb1("vpad", [P, 2, SL * VW])
            vpl = sb1("vpl", [P, P])
            kpl = sb1("kpl", [P, P])
            kd = sb1("kd", [P, P])
            qdm = sb1("qdm", [P, P])
            sblk = sb1("sblk", [P, P])
            htok = sb1("htok", [P, 2, P])
            qm = sb1("qm", [P, 2, SL * P])
            sm = sb1("sm", [P, SL * P])
            oT = sb1("oT", [P, P])
            lt = sb1("lt", [P, P])
            l2 = sb1("l2", [P, P])
            lst = sb1("lst", [P, 8, 2])

            ld_w = sem("ld_w")
            s_zero = sem("s_zero")
            s_pool0 = sem("s_pool0")
            s_set = sem("s_set")
            s_dve0 = sem("s_dve0")
            s_act0 = sem("s_act0")
            s_pe0 = sem("s_pe0")
            x_in = [sem("x_in0"), sem("x_in1")]
            pe_grp = sem("pe_grp")
            kq_done = sem("kq_done")
            cv_done = sem("cv_done")
            var_done = sem("var_done")
            tree_ch = sem("tree_ch")
            act_rs = sem("act_rs")
            rs_done = sem("rs_done")
            s3_done = sem("s3_done")
            ex_done = sem("ex_done")
            aw_done = sem("aw_done")
            pv_done = sem("pv_done")
            soft_ch = sem("soft_ch")
            dred_done = sem("dred_done")
            agg_ch = sem("agg_ch")
            agg_done = sem("agg_done")
            agT_pe = sem("agT_pe")
            agT_ev = sem("agT_ev")
            pj_done = sem("pj_done")
            hT_done = sem("hT_done")
            xs_ch = sem("xs_ch")
            xs_done = sem("xs_done")
            qp_pe = sem("qp_pe")
            qp_ch = sem("qp_ch")
            qv_done = sem("qv_done")
            q_act = sem("q_act")
            qrs_done = sem("qrs_done")
            qp_done = sem("qp_done")
            pe_a = sem("pe_a")
            aev = sem("aev")
            aev_s = sem("aev_s")
            kd_done = sem("kd_done")
            s_pe = sem("s_pe")
            sb_done = sem("sb_done")
            qd_done = sem("qd_done")
            qm_done = sem("qm_done")
            sc_done = sem("sc_done")
            mask_done = sem("mask_done")
            o_done = sem("o_done")
            oT_done = sem("oT_done")
            pr_done = sem("pr_done")
            lnr_done = sem("lnr_done")
            ln_ch = sem("ln_ch")
            lnv_done = sem("lnv_done")
            ln_act = sem("ln_act")
            lrs_done = sem("lrs_done")
            h1_done = sem("h1_done")

            LOADS = 24
            block = early.enter_context(nc.Block())

            xr = x.rearrange("n c (s a b) w -> (n c) s a b w", s=2, b=ST)

            def row(ap, n):
                return ap.unsqueeze(0).to_broadcast([P, n])

            @block.sync
            def _(sp):
                sp.wait_ge(s_zero, 8)
                todo = [
                    (rows[0:64, 0, :], Wq), (rows[64:128, 0, :], Wq),
                    (rows[0:64, 1, :], Wkv[0:64, :]), (rows[64:128, 1, :], Wkv[0:64, :]),
                    (rows[0:64, 2, :], Wkv[64:128, :]), (rows[64:128, 2, :], Wkv[64:128, :]),
                    (rows[0:64, 3, :], proj_w), (rows[64:128, 3, :], proj_w),
                    (lnb[:, 0, :], row(ln_q_w, 64)), (lnb[:, 1, :], row(ln_q_b, 64)),
                    (lnb[:, 2, :], row(ln_kv_w, 64)), (lnb[:, 3, :], row(ln_kv_b, 64)),
                    (bprow64[:], row(b_proj, 64)), (slb[:], row(slopes, 8)),
                ]
                for m in range(2):
                    r = slice(64 * m, 64 * m + 64)
                    todo += [
                        (pb_col[r, :], proj_b.unsqueeze(1)),
                        (w_aq[r, 64 * m:64 * m + 64], w_qkv[:, 0:64]),
                        (w_avki[r, 64 * m:64 * m + 64], w_qkv[:, 128:192]),
                        (w_avki[r, P + 64 * m:P + 64 * m + 64], w_qkv[:, 64:128]),
                        (w_ap[r, 64 * m:64 * m + 64], w_proj),
                    ]
                for dst, src in todo:
                    sp.dma_start(dst, src).then_inc(ld_w, 16)
                assert len(todo) == LOADS

                def load(i, s):
                    sp.wait_ge(pe_grp, done(i, s, 2, NG))
                    for b in range(ST):
                        sp.dma_start(xb[:, s, b * PX // ST:(b + 1) * PX // ST].rearrange("p (a w) -> p a w", w=WW),
                                     xr[bass.ds(i * P, P), s, :, b, :]).then_inc(x_in[s], 16)
                load(0, 0)
                load(0, 1)
                with sp.Fori(1, UNITS // 2) as i:
                    load(i, 0)
                    load(i, 1)

            @block.tensor
            def _(pe):
                pe.wait_ge(s_dve0, 1)
                for j in range(4):
                    nc.tensor.transpose(ps[:, 0, j * P:(j + 1) * P], cat[:, j, :], ident[:])
                for j in range(2):
                    nc.tensor.matmul(ps[:, 1, j * P:(j + 1) * P], ones[:], scr[:, j, :], start=True, stop=True)
                pe.wait_ge(s_act0, 1)
                nc.tensor.transpose(ps[:, 1, 2 * P:3 * P], qd_tok[:], ident[:]).then_inc(s_pe0, 1)
                pe.wait_ge(s_dve0, 2)

                def step(i, s):
                    o = 1 - s
                    if there(i, s, 0):
                        xv = xb[:, s, :].rearrange("p (b k d) -> p b d k", b=ST, d=ST)
                        pe.wait_ge(x_in[s], (i + 1) * 16 * ST)
                        for g in range(NG):
                            if g == 0:
                                pe.wait_ge(kq_done, floor0(done(i, s, 1, NG) - 1))
                                pe.wait_ge(cv_done, floor0(done(i, s, 1, 2 * NG) - 2))
                                pe.wait_ge(mask_done, done(i, s, 4, 4))
                            elif g == 1:
                                pe.wait_ge(kq_done, done(i, s, 1, NG))
                                pe.wait_ge(cv_done, done(i, s, 1, 2 * NG))
                                pe.wait_ge(aev, done(i, s, 3, 4))
                                pe.wait_ge(aev_s, 2 * pairs_done(i, -1 if s == 0 else 0))
                            else:
                                pe.wait_ge(kq_done, floor0(done(i, s, 0, NG) - 5 + g))
                                pe.wait_ge(cv_done, floor0(done(i, s, 0, 2 * NG) - 10 + 2 * g))
                            for j in range(GN):
                                n = g * GN + j
                                px = xv[:, n // ST, n % ST]
                                nc.tensor.matmul(KB[g % 2][:, j * P:(j + 1) * P], px, w_ckv[:, 2 * P:3 * P],
                                                 start=True, stop=True)
                                mm = nc.tensor.matmul(CV[g % 2][:, j * 2 * P:(j + 1) * 2 * P], px,
                                                      w_ckv[:, 0:2 * P], start=True, stop=True)
                            mm.then_inc(pe_grp, 1)
                    if there(i, s, 1):
                        pe.wait_ge(agg_done, done(i, s, 1, 1))
                        pe.wait_ge(qp_done, done(i, s, 0, 1))
                        nc.tensor.transpose(B6[:, 0:P], aggn[:], ident[:]).then_inc(agT_pe, 1)
                    if there(i, s, 2):
                        pe.wait_ge(hT_done, done(i, s, 2, 1))
                        pe.wait_ge(cv_done, done(i, s, 0, 2 * NG))
                        pe.wait_ge(aev, done(i, s, 3, 4))
                        pe.wait_ge(aev_s, 2 * pairs_done(i, -1 if s == 0 else 0))
                        nc.tensor.matmul(QKB[:, 0:P], w_aq[:], hT[:, s, :], start=True, stop=True)
                        nc.tensor.matmul(QKB[:, P:2 * P], w_avki[:, P:2 * P], hT[:, s, :], start=True, stop=True)
                        nc.tensor.matmul(VKB[:, 0:3 * P], hT[:, s, :], w_avki[:], start=True,
                                         stop=True).then_inc(pe_a, 1)
                    if there(i, s, 3):
                        pe.wait_ge(qm_done, done(i, s, 3, 1))
                        pe.wait_ge(aev, done(i, s, 3, 4))
                        pe.wait_ge(mask_done, done(i, s, 4, 4))
                        for r in range(4):
                            if r == 0:
                                pe.wait_ge(kq_done, floor0(done(i, s, 0, NG) - 1))
                            if r == 1:
                                pe.wait_ge(kq_done, done(i, s, 0, NG))
                            if r == 2:
                                pe.wait_ge(cv_done, floor0(done(i, s, 0, 2 * NG) - 2))
                            nc.tensor.matmul(SCB[r], kT[:, o, :], qm[:, o, r * 512:(r + 1) * 512],
                                             start=True, stop=True).then_inc(sc_done, 1)
                    if there(i, s, 2) and s == 0:
                        pe.wait_ge(kd_done, pairs_done(i, 0))
                        pe.wait_ge(agT_ev, done(i, s, 1, 1))
                        pe.wait_ge(qp_done, done(i, s, 0, 1))
                        nc.tensor.matmul(B6[:, 3 * P:4 * P], kd[:], vpl[:], start=True, stop=True).then_inc(s_pe, 1)
                    if there(i, s, 1):
                        pe.wait_ge(agT_ev, done(i, s, 1, 1))
                        nc.tensor.matmul(B6[:, P:2 * P], w_pj[:], aggT[:], start=True, stop=True).then_inc(pj_done, 1)
                    if there(i, s, 3):
                        pe.wait_ge(lnr_done, done(i, s, 4, 1))
                        for j in range(SL):
                            if j % 4 == 0:
                                pe.wait_ge(mask_done, floor0(done(i, s, 3, 4) - 3 + j // 4))
                            mm = nc.tensor.matmul(B7[:, 0:P], vpad[:, o, j * P:(j + 1) * P],
                                                  sm[:, j * P:(j + 1) * P], start=(j == 0),
                                                  stop=(j == SL - 1 and s == 1))
                        if s == 0:
                            pe.wait_ge(sb_done, pairs_done(i, -1))
                            pe.wait_ge(qd_done, pairs_done(i, -1))
                            mm = nc.tensor.matmul(B7[:, 0:P], sblk[:], qdm[:], start=False, stop=True)
                        mm.then_inc(o_done, 1)
                    if there(i, s, -1):
                        pe.wait_ge(xs_done, done(i, s, -1, 1))
                        pe.wait_ge(hT_done, done(i, s, 1, 1))
                        if s == 0:
                            pe.wait_ge(sb_done, pairs_done(i, 0))
                        nc.tensor.matmul(B6[:, 0:2 * P], red[:, o, :], w_q_id[:], start=True,
                                         stop=True).then_inc(qp_pe, 1)
                    if there(i, s, 3):
                        pe.wait_ge(oT_done, done(i, s, 3, 1))
                        nc.tensor.matmul(B7[:, P:2 * P], oT[:], w_ap[:], start=True, stop=True).then_inc(pr_done, 1)
                units(pe, step)

            @block.scalar
            def _(act):
                act.wait_ge(s_dve0, 1)
                for h in range(HEADS):
                    nc.scalar.activation(decay[:, h, :], diff[:], ACT.Exp, scale=nsl[:, h:h + 1])
                nc.scalar.activation(kdec[:], nsl[:], ACT.Exp, scale=pos[:, 1:2])
                nc.scalar.activation(qd_tok[:], scr[:, 2, :], ACT.Exp, scale=pos[:, 0:1]).then_inc(s_act0, 1)
                act.wait_ge(s_dve0, 2)

                def rsqrt_guess(v, y, ready, n, link_sem, base, signal):
                    act.wait_ge(ready, n)
                    nc.scalar.activation(y, v, ACT.Ln, scale=1.0 / C, bias=eps_col[:, 0:1]).then_inc(link_sem, 1)
                    act.wait_ge(link_sem, base)
                    nc.scalar.activation(y, y, ACT.Exp, scale=-0.5).then_inc(signal, 1)

                def step(i, s):
                    o = 1 - s
                    if there(i, s, 0):
                        act.wait_ge(var_done, done(i, s, 2, 1))
                        act.wait_ge(pv_done, done(i, s, 2, 1))
                        for g in range(NG):
                            act.wait_ge(pe_grp, floor0(done(i, s, 0, NG) - 3 + g))
                            cvw = CV[g % 2].rearrange("p (n c) -> p n c", c=2 * P)
                            dst = slice(g * GN * P, (g + 1) * GN * P)
                            nc.scalar.activation(sq[:, s, dst].rearrange("p (n c) -> p n c", c=P),
                                                 cvw[:, :, 0:P], ACT.Square).then_inc(cv_done, 1)
                            nc.scalar.activation(vs[:, s, dst].rearrange("p (n c) -> p n c", c=P),
                                                 cvw[:, :, P:2 * P], ACT.Copy).then_inc(cv_done, 1)
                    if there(i, s, 1):
                        act.wait_ge(agT_pe, done(i, s, 1, 1))
                        act.wait_ge(pj_done, done(i, s, 2, 1))
                        nc.scalar.activation(aggT[:], B6[:, 0:P], ACT.Identity, bias=bv_col[:, 0:1]).then_inc(agT_ev, 1)
                    if there(i, s, 2):
                        act.wait_ge(pe_a, done(i, s, 2, 1))
                        act.wait_ge(sc_done, done(i, s, 4, 4))
                        act.wait_ge(qm_done, done(i, s, 4, 1))
                        act.wait_ge(o_done, done(i, s, 4, 1))
                        act.wait_ge(lnr_done, done(i, s, 4, 1))
                        nc.scalar.activation(qT[:, s, :], QKB[:, 0:P], ACT.Copy, scale=ATT_SCALE).then_inc(aev, 1)
                        nc.scalar.activation(kT[:, s, :], QKB[:, P:2 * P], ACT.Copy).then_inc(aev, 1)
                        nc.scalar.activation(
                            vpad[:, s, :].rearrange("p (j w) -> p j w", w=VW)[:, :, 0:D],
                            VKB[:, 0:P].rearrange("p (j d) -> p j d", d=D), ACT.Copy).then_inc(aev, 1)
                        if s == 0:
                            act.wait_ge(s_pe, pairs_done(i, -1))
                            nc.scalar.activation(vpl[:], VKB[:, 0:P], ACT.Copy).then_inc(aev_s, 1)
                            nc.scalar.activation(kpl[:], VKB[:, P:2 * P], ACT.Copy).then_inc(aev_s, 1)
                        nc.scalar.activation(htok[:, s, :], VKB[:, 2 * P:3 * P], ACT.Copy).then_inc(aev, 1)
                    if there(i, s, 4):
                        rsqrt_guess(lst[:, 4, :], lst[:, 3, :], lnv_done, done(i, s, 4, 1), ln_act,
                                    done(i, s, 4, 1), lrs_done)
                    if there(i, s, 0):
                        act.wait_ge(aw_done, done(i, s, 1, 1))
                        rsqrt_guess(ssq[:, s, :], yrs[:], var_done, done(i, s, 0, 1), act_rs,
                                    done(i, s, 0, 1), rs_done)
                        act.wait_ge(s3_done, done(i, s, 0, 1))
                        nc.scalar.activation(ex[:], sc[:], ACT.Exp, scale=TOK_SCALE).then_inc(ex_done, 1)
                    if there(i, s, 3):
                        act.wait_ge(o_done, done(i, s, 3, 1))
                        act.wait_ge(pr_done, done(i, s, 4, 1))
                        nc.scalar.activation(oT[:], B7[:, 0:P], ACT.Copy).then_inc(oT_done, 1)
                    if there(i, s, -1):
                        rsqrt_guess(qst[:, 4, :], qst[:, 3, :], qv_done, done(i, s, -1, 1), q_act,
                                    done(i, s, -1, 1), qrs_done)
                units(act, step)

            @block.gpsimd
            def _(pool):
                for t in (w_aq, w_ap, w_avki, vpad, ident, blockmask):
                    nc.gpsimd.memset(t[:], 0.0).then_inc(s_zero, 1)
                nc.gpsimd.memset(ones[:], 1.0).then_inc(s_zero, 1)
                nc.gpsimd.memset(headmask[:], 1.0).then_inc(s_zero, 1)
                nc.gpsimd.iota(diffi[:], pattern=[[1, P]], base=0, channel_multiplier=-1).then_inc(s_pool0, 1)
                nc.gpsimd.iota(posi[:], pattern=[[0, 1]], base=0, channel_multiplier=1).then_inc(s_pool0, 1)
                link, n = chain(pool, s_pool0, 2)
                pool.wait_ge(s_pool0, 2)
                pool.wait_ge(s_zero, 8)
                link(nc.gpsimd.affine_select(out=ident[:], in_=ident[:], compare_op=ALU.not_equal, fill=1.0, base=0,
                                             pattern=[[-1, P]], channel_multiplier=1))
                for m in range(2):
                    link(nc.gpsimd.memset(blockmask[64 * m:64 * m + 64, 64 * m:64 * m + 64], 1.0))
                for base, pattern, step_p in ((0, [[-D, SL]], 1), (D - 1, [[D, SL]], -1)):
                    link(nc.gpsimd.affine_select(out=headmask[:], in_=headmask[:], compare_op=ALU.is_ge, fill=0.0,
                                                 base=base, pattern=pattern, channel_multiplier=step_p))

                def step(i, s):
                    o = 1 - s
                    if there(i, s, 0):
                        link, n = chain(pool, tree_ch, done(i, s, 1, 5))
                        pool.wait_ge(cv_done, done(i, s, 0, 2 * NG))
                        pool.wait_ge(aw_done, done(i, s, 2, 1))
                        v = sq[:, s, :].rearrange("p (n c) -> p n c", c=C)
                        w = C // 2
                        while w > 1:
                            link(nc.gpsimd.tensor_tensor(v[:, :, 0:w], v[:, :, 0:w], v[:, :, w:2 * w], ALU.add))
                            w //= 2
                        nc.gpsimd.tensor_tensor(ssq[:, s, :].unsqueeze(2), v[:, :, 0:1], v[:, :, 1:2],
                                                ALU.add).then_inc(var_done, 1)
                    if there(i, s, 2):
                        pool.wait_ge(aev, done(i, s, 2, 4))
                        pool.wait_ge(sc_done, done(i, s, 4, 4))
                        nc.gpsimd.tensor_tensor(
                            qm[:, s, :].rearrange("p (j c) -> p j c", c=P),
                            qT[:, s, :].unsqueeze(1).to_broadcast([P, SL, P]),
                            headmask[:].unsqueeze(2).to_broadcast([P, SL, P]), ALU.mult).then_inc(qm_done, 1)
                    if there(i, s, 0):
                        pool.wait_ge(aw_done, done(i, s, 0, 1))
                        nc.gpsimd.tensor_tensor(
                            pv[:].rearrange("p (k d) -> p k d", d=D),
                            vs[:, s, :].rearrange("p (k d) -> p k d", d=D),
                            aw[:].unsqueeze(2).to_broadcast([P, N * SL, D]), ALU.mult).then_inc(pv_done, 1)
                units(pool, step)

            @block.vector
            def _(dve):
                dve.wait_ge(s_pool0, 7)
                dve.wait_ge(ld_w, 16 * LOADS)
                link, n = chain(dve, s_set, 0)
                V = nc.vector
                link(V.memset(eps_col[:], EPS))
                link(V.tensor_copy(diff[:], diffi[:]))
                link(V.tensor_scalar(tril[:], diff[:], 0.0, None, ALU.is_ge))
                link(V.tensor_scalar(diff[:], diff[:], 0.0, None, ALU.max))
                link(V.tensor_copy(pos[:, 0:1], posi[:]))
                link(V.tensor_scalar(pos[:, 1:2], pos[:, 0:1], -1.0, float(P), ALU.mult, ALU.add))
                link(V.tensor_scalar(nsl[:], slb[:], -1.0, None, ALU.mult))
                for m in range(2):
                    link(V.tensor_copy(scr[:, 2, m * C:(m + 1) * C].rearrange("p (h d) -> p h d", d=D),
                                       nsl[:].unsqueeze(2).to_broadcast([P, HEADS, D])))
                    link(V.tensor_copy(bp_row[:, m * C:(m + 1) * C], bprow64[:]))
                for j, b_at, dst in ((0, 1, col[:, 0:1]), (1, 3, col[:, 1:2]), (2, 3, bv_col[:])):
                    link(V.tensor_tensor(scr[:, 3, 0:C], rows[:, j, :], lnb[:, b_at, :], ALU.mult))
                    link(V.tensor_reduce(dst, scr[:, 3, 0:C], AX, ALU.add))
                for j, g_at in ((0, 0), (1, 2), (2, 2)):
                    link(V.tensor_tensor(rows[:, j, :], rows[:, j, :], lnb[:, g_at, :], ALU.mult))
                    link(V.tensor_reduce(col[:, 2:3], rows[:, j, :], AX, ALU.add))
                    link(V.tensor_scalar(col[:, 3:4], col[:, 2:3], -1.0 / C, None, ALU.mult))
                    link(V.tensor_scalar(rows[:, j, :], rows[:, j, :], col[:, 3:4], None, ALU.add))
                for j in range(4):
                    for m in range(2):
                        link(V.tensor_copy(cat[:, j, m * C:(m + 1) * C], rows[:, j, :]))
                link(V.tensor_scalar(scr[:, 0, :], ident[:], col[:, 0:1], None, ALU.mult))
                link(V.tensor_scalar(scr[:, 1, :], ident[:], col[:, 1:2], None, ALU.mult))
                link(V.tensor_scalar(ident2[:], ident[:], 2.0, None, ALU.mult))
                link(V.scalar_tensor_tensor(w_ckv[:, 0:P], blockmask[:], -1.0 / C, ident[:], ALU.mult, ALU.add))
                link(V.tensor_copy(w_q_id[:, P:2 * P], ident[:]))
                V.tensor_copy(w_avki[:, 2 * P:3 * P], ident[:]).then_inc(s_dve0, 1)
                dve.wait_ge(s_pe0, 1)
                for j, dst in ((0, w_q_id[:, 0:P]), (1, w_ckv[:, 2 * P:3 * P]), (2, w_ckv[:, P:2 * P]), (3, w_pj[:])):
                    link(V.tensor_tensor(dst, ps[:, 0, j * P:(j + 1) * P], blockmask[:], ALU.mult))
                link(V.tensor_copy(bq_row[:], ps[:, 1, 0:P]))
                link(V.tensor_copy(bk_row[:], ps[:, 1, P:2 * P]))
                link(V.tensor_copy(qdec[:], ps[:, 1, 2 * P:3 * P]))
                V.tensor_tensor(decay[:], decay[:], tril[:].unsqueeze(1).to_broadcast([P, HEADS, P]),
                                ALU.mult).then_inc(s_dve0, 1)
                dve.wait_ge(s_dve0, 2)

                def newton(link, y, v, t):
                    link(V.tensor_tensor(t, y, y, ALU.mult))
                    link(V.tensor_tensor(t, t, v, ALU.mult))
                    link(V.tensor_scalar(t, t, -0.5, 1.5, ALU.mult, ALU.add))
                    link(V.tensor_tensor(y, y, t, ALU.mult))

                def heads(ap):
                    return ap.rearrange("p (m c) -> p m c", c=C)

                def step(i, s):
                    o = 1 - s
                    if there(i, s, 0):
                        for g in range(NG):
                            dve.wait_ge(pe_grp, floor0(done(i, s, 0, NG) - 3 + g))
                            V.tensor_tensor(kq[:, g * GN * P:(g + 1) * GN * P].rearrange("p (n c) -> p n c", c=P),
                                            KB[g % 2].rearrange("p (n c) -> p n c", c=P),
                                            qq[:].unsqueeze(1).to_broadcast([P, GN, P]),
                                            ALU.mult).then_inc(kq_done, 1)
                    if there(i, s, 4):
                        link_l, nl = chain(dve, ln_ch, done(i, s, 5, 11))
                        link_l(V.tensor_tensor(lt[:], lt[:], bp_row[:], ALU.add))
                        link_l(V.tensor_reduce(lst[:, 0, :], heads(lt[:]), AX, ALU.add))
                        link_l(V.tensor_scalar(lst[:, 1, :], lst[:, 0, :], -1.0 / C, None, ALU.mult))
                        link_l(V.tensor_tensor(heads(lt[:]), heads(lt[:]),
                                               lst[:, 1, :].unsqueeze(2).to_broadcast([P, 2, C]), ALU.add))
                        link_l(V.tensor_tensor(l2[:], lt[:], lt[:], ALU.mult))
                        V.tensor_reduce(lst[:, 4, :], heads(l2[:]), AX, ALU.add).then_inc(lnv_done, 1)
                        dve.wait_ge(lnv_done, done(i, s, 4, 1))
                        link_l(V.tensor_scalar(lst[:, 2, :], lst[:, 4, :], 1.0 / C, EPS, ALU.mult, ALU.add))
                    if there(i, s, 1):
                        link, n = chain(dve, agg_ch, done(i, s, 2, 1))
                        dve.wait_ge(pv_done, done(i, s, 1, 1))
                        link(V.tensor_reduce(agg[:], pv[:].rearrange("p (n c) -> p c n", c=P), AX, ALU.add))
                        dve.wait_ge(agT_pe, done(i, s, 2, 1))
                        V.tensor_tensor(aggn[:].rearrange("p (j d) -> p j d", d=D),
                                        agg[:].rearrange("p (j d) -> p j d", d=D),
                                        rden[:].unsqueeze(2).to_broadcast([P, SL, D]), ALU.mult).then_inc(agg_done, 1)
                    if there(i, s, 0):
                        dve.wait_ge(kq_done, done(i, s, 0, NG))
                        V.tensor_reduce(sc[:], kq[:].rearrange("p (k d) -> p k d", d=D), AX,
                                        ALU.add).then_inc(dred_done, 1)
                    if there(i, s, 4):
                        dve.wait_ge(lrs_done, done(i, s, 4, 1))
                        newton(link_l, lst[:, 3, :], lst[:, 2, :], lst[:, 6, :])
                        assert nl[0] == 10
                        V.tensor_tensor(h1[:, bass.ds(2 * i + s - 4, 1), :].rearrange("p u (m c) -> p (u m) c", c=C),
                                        heads(lt[:]), lst[:, 3, :].unsqueeze(2).to_broadcast([P, 2, C]),
                                        ALU.mult).then_inc(ln_ch, 1)
                    if there(i, s, 0):
                        link, n = chain(dve, soft_ch, done(i, s, 1, 10))
                        dve.wait_ge(var_done, done(i, s, 0, 1))
                        link(V.tensor_scalar(var[:], ssq[:, s, :], 1.0 / C, EPS, ALU.mult, ALU.add))
                        dve.wait_ge(rs_done, done(i, s, 0, 1))
                        newton(link, yrs[:], var[:], yt[:])
                        dve.wait_ge(dred_done, done(i, s, 0, 1))
                        dve.wait_ge(qp_done, done(i, s, 0, 1))
                        s3 = sc[:].rearrange("p (k h) -> p k h", h=HEADS)
                        sn = sc[:].rearrange("p (n j) -> p n j", j=SL)
                        rs_b = yrs[:].unsqueeze(2).to_broadcast([P, 2 * N, HEADS])
                        link(V.tensor_tensor(s3, s3, rs_b, ALU.mult))
                        link(V.tensor_tensor(sn, sn, sbias[:].unsqueeze(1).to_broadcast([P, N, SL]), ALU.add))
                        link(V.tensor_reduce(mx[:], sc[:].rearrange("p (n j) -> p j n", j=SL), AX, ALU.max))
                        V.tensor_tensor(sn, sn, mx[:].unsqueeze(1).to_broadcast([P, N, SL]),
                                        ALU.subtract).then_inc(s3_done, 1)
                    if there(i, s, 2) and s == 0:
                        dve.wait_ge(aev_s, 2 * pairs_done(i, 0))
                        dve.wait_ge(s_pe, pairs_done(i, -1))
                        V.tensor_tensor(kd[:].rearrange("p (m h d) -> p m h d", m=2, d=D),
                                        kpl[:].rearrange("p (m h d) -> p m h d", m=2, d=D),
                                        kdec[:].unsqueeze(1).unsqueeze(3).to_broadcast([P, 2, HEADS, D]),
                                        ALU.mult).then_inc(kd_done, 1)
                    if there(i, s, 3) and s == 0:
                        dve.wait_ge(aev, done(i, s, 3, 4))
                        dve.wait_ge(o_done, done(i, s, 5, 1))
                        V.tensor_tensor(qdm[:], qT[:, o, :], qdec[:], ALU.mult).then_inc(qd_done, 1)
                    if there(i, s, 0):
                        dve.wait_ge(ex_done, done(i, s, 0, 1))
                        link(V.tensor_reduce(den[:], ex[:].rearrange("p (n j) -> p j n", j=SL), AX, ALU.add))
                        link(V.reciprocal(rden[:], den[:]))
                        V.tensor_tensor(aw[:].rearrange("p (k h) -> p k h", h=HEADS),
                                        ex[:].rearrange("p (k h) -> p k h", h=HEADS), rs_b,
                                        ALU.mult).then_inc(aw_done, 1)
                        assert n[0] == 10, n
                    if there(i, s, 3):
                        dve.wait_ge(o_done, done(i, s, 4, 1))
                        for r in range(4):
                            dve.wait_ge(sc_done, floor0(done(i, s, 3, 4) - 3 + r))
                            V.tensor_tensor(sm[:, r * 512:(r + 1) * 512].rearrange("p (h c) -> p h c", c=P),
                                            SCB[r].rearrange("p (h c) -> p h c", c=P),
                                            decay[:, 4 * (r % 2):4 * (r % 2) + 4, :], ALU.mult).then_inc(mask_done, 1)
                    if there(i, s, 1):
                        dve.wait_ge(pj_done, done(i, s, 1, 1))
                        dve.wait_ge(pe_a, done(i, s, 3, 1))
                        V.scalar_tensor_tensor(hT[:, o, :], B6[:, P:2 * P], pb_col[:, 0:1], red[:, o, :],
                                               ALU.add, ALU.add).then_inc(hT_done, 1)
                    if there(i, s, 2) and s == 0:
                        dve.wait_ge(s_pe, pairs_done(i, 0))
                        dve.wait_ge(o_done, done(i, s, 3, 1))
                        V.tensor_tensor(sblk[:].rearrange("p (j d) -> p j d", d=D),
                                        B6[:, 3 * P:4 * P].rearrange("p (j d) -> p j d", d=D),
                                        headmask[:].unsqueeze(2).to_broadcast([P, SL, D]),
                                        ALU.mult).then_inc(sb_done, 1)
                    if there(i, s, -1):
                        link, n = chain(dve, xs_ch, done(i, s, 0, 1))
                        dve.wait_ge(x_in[o], floor0(16 * ST * (i + 1 if s == 0 else i + 2)))
                        link(V.tensor_reduce(rsum[:],
                                             xb[:, o, :].rearrange("p (b k d) -> p k b d", b=ST, d=ST),
                                             mybir.AxisListType.XY, ALU.add))
                        dve.wait_ge(qp_pe, done(i, s, 1, 1))
                        V.tensor_scalar(red[:, o, :], rsum[:], 1.0 / N, None, ALU.mult).then_inc(xs_done, 1)
                    if there(i, s, 3):
                        dve.wait_ge(pr_done, done(i, s, 3, 1))
                        dve.wait_ge(ln_ch, done(i, s, 4, 11))
                        V.tensor_tensor(lt[:], B7[:, P:2 * P], htok[:, o, :], ALU.add).then_inc(lnr_done, 1)
                        dve.wait_ge(lnr_done, done(i, s, 3, 1))
                    if there(i, s, -1):
                        link, n = chain(dve, qp_ch, done(i, s, 0, 12))
                        dve.wait_ge(qp_pe, done(i, s, -1, 1))
                        rt = heads(B6[:, P:2 * P])
                        link(V.tensor_reduce(qst[:, 0, :], rt, AX, ALU.add))
                        link(V.tensor_scalar(qst[:, 1, :], qst[:, 0, :], -1.0 / C, None, ALU.mult))
                        link(V.tensor_tensor(heads(qc[:]), rt, qst[:, 1, :].unsqueeze(2).to_broadcast([P, 2, C]),
                                             ALU.add))
                        link(V.tensor_tensor(q2[:], qc[:], qc[:], ALU.mult))
                        V.tensor_reduce(qst[:, 4, :], heads(q2[:]), AX, ALU.add).then_inc(qv_done, 1)
                        dve.wait_ge(qv_done, done(i, s, -1, 1))
                        link(V.tensor_scalar(qst[:, 2, :], qst[:, 4, :], 1.0 / C, EPS, ALU.mult, ALU.add))
                        dve.wait_ge(qrs_done, done(i, s, -1, 1))
                        newton(link, qst[:, 3, :], qst[:, 2, :], qst[:, 6, :])
                        link(V.tensor_tensor(heads(q2[:]), heads(B6[:, 0:P]),
                                             qst[:, 3, :].unsqueeze(2).to_broadcast([P, 2, C]), ALU.mult))
                        link(V.tensor_tensor(qq[:], q2[:], bq_row[:], ALU.add))
                        link(V.tensor_tensor(qc[:], qq[:], bk_row[:], ALU.mult))
                        assert n[0] == 12, n
                        V.tensor_reduce(sbias[:], qc[:].rearrange("p (j d) -> p j d", d=D), AX,
                                        ALU.add).then_inc(qp_done, 1)
                units(dve, step)

        G = UNITS // 4
        with ExitStack() as late:
            def sb2(name, shape, dt=F32):
                return late.enter_context(nc.sbuf_tensor(name, shape, dt))

            w1bd = sb2("w1bd", [P, E, P])
            w2bd = sb2("w2bd", [P, E, P])
            rt = sb2("rt", [P, 2 * E])
            b1c = sb2("b1c", [P, E])
            b2v = sb2("b2v", [P, 4, P])
            lg = sb2("lg", [P, 2 * UNITS, E])
            ra = sb2("ra", [P, 2 * UNITS, E])
            rb = sb2("rb", [P, 2 * UNITS, E])
            comb = sb2("comb", [P, 2 * UNITS, E])
            r1 = sb2("r1", [P, 2 * UNITS])
            r2 = sb2("r2", [P, 2 * UNITS])
            rank = sb2("rank", [P, E])
            st = sb2("st", [P, 2, 4 * P])
            tokT = sb2("tokT", [P, 2, 4 * P])
            cb = sb2("cb", [P, 2, P])
            cbT = sb2("cbT", [P, 2, P])
            hid = sb2("hid", [P, 2, E, 4 * P])
            pr = sb2("pr", [P, E, P])
            y = sb2("y", [P, 4 * P])
            y2 = sb2("y2", [P, 4 * P])
            nst = sb2("nst", [P, 8, 8])
            nsi = sb2("nsi", [P, 8], I32)
            outb = sb2("outb", [P, 2, 4 * P])

            ld2 = sem("ld2")
            z2 = sem("z2")
            st_a = sem("st_a")
            tr_a = sem("tr_a")
            tv_a = sem("tv_a")
            lg_pe = sem("lg_pe")
            lg_done = sem("lg_done")
            rt_ch = sem("rt_ch")
            rt_sub = sem("rt_sub")
            rt_exp = sem("rt_exp")
            comb_done = sem("comb_done")
            st_b = sem("st_b")
            tr_b = sem("tr_b")
            tv_b = sem("tv_b")
            up_done = sem("up_done")
            gelu_done = sem("gelu_done")
            dn_done = sem("dn_done")
            x0_done = sem("x0_done")
            pr_read = sem("pr_read")
            x0_read = sem("x0_read")
            y_ch = sem("y_ch")
            y_done = sem("y_done")
            out_done = [sem("out_done0"), sem("out_done1")]

            def gdone(i, s, lag, per):
                if isinstance(i, int):
                    return max(0, min(G, 2 * i + s - lag + 1)) * per
                return i * (2 * per) + (s - lag + 1) * per

            def gthere(i, s, lag):
                return not isinstance(i, int) or 0 <= 2 * i + s - lag < G

            def groups(eng, step):
                for i in (0, 1):
                    step(i, 0)
                    step(i, 1)
                with eng.Fori(2, G // 2 - 1) as i:
                    step(i, 0)
                    step(i, 1)
                step(G // 2 - 1, 0)
                step(G // 2 - 1, 1)
                step(G // 2, 0)

            block2 = late.enter_context(nc.Block())
            LOADS2 = 16

            @block2.gpsimd
            def _(pool):
                for t in (w1bd, w2bd, rt, b2v, cb):
                    nc.gpsimd.memset(t[:], 0.0).then_inc(z2, 1)
                for e in range(E):
                    nc.gpsimd.memset(rank[:, e:e + 1], float(E - e)).then_inc(z2, 1)

            @block2.sync
            def _(sp):
                sp.wait_ge(z2, 5 + E)
                todo = []
                for m in range(2):
                    r = slice(64 * m, 64 * m + 64)
                    todo += [(w1bd[r, :, r], w1.rearrange("e i o -> i e o")),
                             (w2bd[r, :, r], w2.rearrange("e i o -> i e o")),
                             (rt[r, m * E:(m + 1) * E], router_w.rearrange("e c -> c e")),
                             (b1c[r, :], b1.rearrange("e c -> c e"))]
                    todo += [(b2v[k * 2 * E + m * E:k * 2 * E + (m + 1) * E, k, r], b2) for k in range(4)]
                assert len(todo) == LOADS2
                for dst, src in todo:
                    sp.dma_start(dst, src, allow_slow_non_contiguous=True).then_inc(ld2, 16)

                def store(i, s):
                    sp.wait_ge(y_done, gdone(i, s, 0, 1))
                    for a in range(2):
                        for c in range(2):
                            k = 2 * a + c
                            sp.dma_start(out[bass.ds(i * 8 + 4 * s + 2 * a, 2), c * P:(c + 1) * P, :].rearrange(
                                "m p d -> p m d"), outb[:, s, k * P:(k + 1) * P].rearrange(
                                "p (m d) -> p m d", m=2)).then_inc(out_done[s], 16)
                with sp.Fori(0, G // 2) as i:
                    store(i, 0)
                    store(i, 1)
                for s in range(2):
                    sp.wait_ge(out_done[s], G // 2 * 64)

            @block2.tensor
            def _(pe):
                pe.wait_ge(ld2, 16 * LOADS2)

                def logits(i, s):
                    pe.wait_ge(st_a, gdone(i, s, 0, 1))
                    pe.wait_ge(tv_a, gdone(i, s, 2, 1))
                    for k in range(4):
                        mm = nc.tensor.transpose(ps[:, s, k * P:(k + 1) * P], st[:, s, k * P:(k + 1) * P], ident[:])
                    mm.then_inc(tr_a, 1)
                    pe.wait_ge(tv_a, gdone(i, s, 0, 1))
                    pe.wait_ge(lg_done, gdone(i, s, 2, 1))
                    for k in range(4):
                        mm = nc.tensor.matmul(ps[:, 2 + s, k * 2 * E:(k + 1) * 2 * E],
                                              tokT[:, s, k * P:(k + 1) * P], rt[:], start=True, stop=True)
                    mm.then_inc(lg_pe, 1)
                logits(0, 0)
                logits(0, 1)
                with pe.Fori(1, G // 2) as i:
                    logits(i, 0)
                    logits(i, 1)

                def turn(i, s):
                    pe.wait_ge(st_b, gdone(i, s, 0, 2))
                    pe.wait_ge(tv_b, gdone(i, s, 1, 2))
                    for k in range(4):
                        nc.tensor.transpose(ps[:, 0, k * P:(k + 1) * P], st[:, s, k * P:(k + 1) * P], ident[:])
                    nc.tensor.transpose(ps[:, 1, 0:P], cb[:, s, :], ident[:]).then_inc(tr_b, 1)

                def step(i, s):
                    o = 1 - s
                    if gthere(i, s, 0):
                        turn(i, s)
                    for e in range(E):
                        if gthere(i, s, 0):
                            if e == 0:
                                pe.wait_ge(tv_b, gdone(i, s, 0, 2))
                            pe.wait_ge(gelu_done, floor0(gdone(i, s, 1, E) + e - 1))
                            nc.tensor.matmul(ps[:, 2 + e % 2, :], w1bd[:, e, :], tokT[:, s, :], start=True,
                                             stop=True).then_inc(up_done, 1)
                        if gthere(i, s, 1):
                            k, f = e // 2, e % 2
                            if e == 0:
                                pe.wait_ge(gelu_done, gdone(i, s, 1, E))
                            pe.wait_ge(pr_read, floor0(gdone(i, s, 2, 8) + e - 1))
                            for q in range(4):
                                mm = nc.tensor.matmul(ps[:, 4 + f, q * P:(q + 1) * P],
                                                      hid[:, o, 4 * f + q, k * P:(k + 1) * P],
                                                      w2bd[:, 4 * f + q, :], start=True, stop=True)
                            mm.then_inc(dn_done, 1)
                            if f == 1:
                                pe.wait_ge(x0_read, floor0(gdone(i, s, 2, 4) + k - 1))
                                nc.tensor.matmul(ps[:, 6 + k % 2, 0:P], cbT[:, o, :], b2v[:, k, :],
                                                 start=True, stop=False)
                                nc.tensor.matmul(ps[:, 6 + k % 2, 0:P], tokT[:, o, k * P:(k + 1) * P], ident2[:],
                                                 start=False, stop=True).then_inc(x0_done, 1)
                groups(pe, step)

            @block2.scalar
            def _(act):
                act.wait_ge(z2, 5 + E)

                def logits(i, s):
                    act.wait_ge(tr_a, gdone(i, s, 2, 1))
                    nc.scalar.activation(st[:, s, :].rearrange("p (k c) -> p k c", c=P),
                                         h1[:, bass.ds(i * 8 + 4 * s, 4), :], ACT.Copy).then_inc(st_a, 1)

                def logits_out(i, s):
                    act.wait_ge(tr_a, gdone(i, s, 0, 1))
                    act.wait_ge(lg_pe, gdone(i, s, 2, 1))
                    nc.scalar.activation(tokT[:, s, :], ps[:, s, :], ACT.Copy).then_inc(tv_a, 1)
                    act.wait_ge(lg_pe, gdone(i, s, 0, 1))
                    nc.scalar.activation(lg[:, bass.ds(i * 16 + 8 * s, 8), :],
                                         ps[:, 2 + s, 0:8 * E].rearrange("p (t e) -> p t e", e=E),
                                         ACT.Copy).then_inc(lg_done, 1)
                logits(0, 0)
                logits(0, 1)
                for s in range(2):
                    logits_out(0, s)
                    logits(1, s)
                with act.Fori(1, G // 2 - 1) as i:
                    for s in range(2):
                        logits_out(i, s)
                        logits(i + 1, s)
                logits_out(G // 2 - 1, 0)
                logits_out(G // 2 - 1, 1)
                act.wait_ge(rt_sub, 1)
                nc.scalar.activation(lg[:], lg[:], ACT.Exp).then_inc(rt_exp, 1)

                def stage(i, s):
                    if s == 0 and isinstance(i, int) and i == 0:
                        act.wait_ge(comb_done, 1)
                    act.wait_ge(tr_b, gdone(i, s, 2, 1))
                    nc.scalar.activation(st[:, s, :].rearrange("p (k c) -> p k c", c=P),
                                         h1[:, bass.ds(i * 8 + 4 * s, 4), :], ACT.Copy).then_inc(st_b, 1)
                    act.wait_ge(pr_read, gdone(i, s, 2, 8))
                    nc.scalar.activation(cb[:, s, 0:8 * E].rearrange("p (t e) -> p t e", e=E),
                                         comb[:, bass.ds(i * 16 + 8 * s, 8), :], ACT.Copy).then_inc(st_b, 1)

                def step(i, s):
                    if gthere(i, s, 0):
                        stage(i, s)
                        act.wait_ge(tr_b, gdone(i, s, 0, 1))
                        act.wait_ge(x0_done, gdone(i, s, 2, 4))
                        nc.scalar.activation(tokT[:, s, :], ps[:, 0, :], ACT.Copy).then_inc(tv_b, 1)
                        nc.scalar.activation(cbT[:, s, :], ps[:, 1, 0:P], ACT.Copy).then_inc(tv_b, 1)
                        act.wait_ge(dn_done, gdone(i, s, 2, 8))
                        for e in range(E):
                            act.wait_ge(up_done, floor0(gdone(i, s, 0, E) - E + 1 + e))
                            nc.scalar.activation(hid[:, s, e, :], ps[:, 2 + e % 2, :], ACT.Gelu,
                                                 bias=b1c[:, e:e + 1]).then_inc(gelu_done, 1)
                groups(act, step)

            @block2.vector
            def _(dve):
                V = nc.vector
                dve.wait_ge(z2, 5 + E)
                dve.wait_ge(lg_done, G)
                T = 2 * UNITS
                link, n = chain(dve, rt_ch, 0)

                def over_e(ap):
                    return ap.unsqueeze(2).to_broadcast([P, T, E])

                rank_b = rank[:].unsqueeze(1).to_broadcast([P, T, E])
                link(V.tensor_reduce(r1[:], lg[:], AX, ALU.max))
                V.tensor_tensor(lg[:], lg[:], over_e(r1[:]), ALU.subtract).then_inc(rt_sub, 1)
                dve.wait_ge(rt_exp, 1)
                link(V.tensor_reduce(r1[:], lg[:], AX, ALU.add))
                link(V.reciprocal(r2[:], r1[:]))
                link(V.tensor_tensor(lg[:], lg[:], over_e(r2[:]), ALU.mult))

                def first_largest(src, hot):
                    link(V.tensor_reduce(r1[:], src, AX, ALU.max))
                    link(V.tensor_tensor(hot, src, over_e(r1[:]), ALU.is_equal))
                    link(V.tensor_tensor(hot, hot, rank_b, ALU.mult))
                    link(V.tensor_reduce(r2[:], hot, AX, ALU.max))
                    link(V.tensor_tensor(hot, hot, over_e(r2[:]), ALU.is_equal))
                first_largest(lg[:], ra[:])
                link(V.scalar_tensor_tensor(comb[:], ra[:], -2.0, lg[:], ALU.mult, ALU.add))
                first_largest(comb[:], rb[:])
                link(V.tensor_tensor(ra[:], ra[:], rb[:], ALU.add))
                link(V.tensor_tensor(lg[:], lg[:], ra[:], ALU.mult))
                link(V.tensor_reduce(r1[:], lg[:], AX, ALU.add))
                link(V.tensor_scalar(r1[:], r1[:], 1e-12, None, ALU.max))
                link(V.reciprocal(r2[:], r1[:]))
                V.tensor_tensor(comb[:], lg[:], over_e(r2[:]), ALU.mult).then_inc(comb_done, 1)

                def per_token(ap):
                    return ap.rearrange("p (t c) -> p t c", c=C)

                def step(i, s):
                    o = 1 - s
                    if not gthere(i, s, 1):
                        return
                    YCH = 4 + 6 + 2 + 16
                    link, n = chain(dve, y_ch, gdone(i, s, 2, YCH))
                    dve.wait_ge(st_b, gdone(i, s, 1, 2))
                    for k in range(4):
                        for f in range(2):
                            j = 2 * k + f
                            dve.wait_ge(dn_done, floor0(gdone(i, s, 1, 8) - 7 + j))
                            wv = cb[:, o, k * 2 * E:(k + 1) * 2 * E].rearrange("p (m e) -> p e m", e=E)
                            ins = V.tensor_tensor(
                                pr[:, 4 * f:4 * f + 4, :].rearrange("p e (m c) -> p e m c", c=C),
                                ps[:, 4 + f, :].rearrange("p (e m c) -> p e m c", e=4, c=C),
                                wv[:, 4 * f:4 * f + 4, :].unsqueeze(3).to_broadcast([P, 4, 2, C]), ALU.mult)
                            ins.then_inc(pr_read, 1)
                        dve.wait_ge(pr_read, floor0(gdone(i, s, 1, 8) - 6 + 2 * k))
                        link(V.tensor_reduce(y[:, k * P:(k + 1) * P], pr[:].rearrange("p e c -> p c e"), AX, ALU.add))
                        dve.wait_ge(x0_done, floor0(gdone(i, s, 1, 4) - 3 + k))
                        ins = V.tensor_tensor(y[:, k * P:(k + 1) * P], ps[:, 6 + k % 2, 0:P],
                                              y[:, k * P:(k + 1) * P], ALU.add)
                        ins.then_inc(x0_read, 1)
                        dve.wait_ge(x0_read, floor0(gdone(i, s, 1, 4) - 3 + k))
                    v, t, yy = nst[:, 2, :], nst[:, 3, :], nst[:, 4, :]
                    link(V.tensor_reduce(nst[:, 0, :], per_token(y[:]), AX, ALU.add))
                    link(V.tensor_scalar(nst[:, 1, :], nst[:, 0, :], -1.0 / C, None, ALU.mult))
                    link(V.tensor_tensor(per_token(y[:]), per_token(y[:]),
                                         nst[:, 1, :].unsqueeze(2).to_broadcast([P, 8, C]), ALU.add))
                    link(V.tensor_tensor(y2[:], y[:], y[:], ALU.mult))
                    link(V.tensor_reduce(nst[:, 0, :], per_token(y2[:]), AX, ALU.add))
                    link(V.tensor_scalar(v, nst[:, 0, :], 1.0 / C, EPS, ALU.mult, ALU.add))
                    link(V.tensor_scalar(nsi[:], v.bitcast(I32), 1, None, ALU.logical_shift_right))
                    link(V.tensor_scalar(yy.bitcast(I32), nsi[:], -1.0, float(0x5f3759df), ALU.mult, ALU.add))
                    for _ in range(4):
                        link(V.tensor_tensor(t, yy, yy, ALU.mult))
                        link(V.tensor_tensor(t, t, v, ALU.mult))
                        link(V.tensor_scalar(t, t, -0.5, 1.5, ALU.mult, ALU.add))
                        link(V.tensor_tensor(yy, yy, t, ALU.mult))
                    assert n[0] == YCH, n
                    dve.wait_ge(out_done[o], 64 * out_before(i, s))
                    V.tensor_tensor(per_token(outb[:, o, :]), per_token(y[:]),
                                    yy.unsqueeze(2).to_broadcast([P, 8, C]), ALU.mult).then_inc(y_done, 1)

                def out_before(i, s):
                    return i - 1 if s == 0 else i
                groups(dve, step)


_INS = ['x', 'L0_tok_ln_q_w', 'L0_tok_ln_q_b', 'L0_tok_Wq', 'L0_tok_ln_kv_w', 'L0_tok_ln_kv_b', 'L0_tok_Wkv',
        'L0_tok_proj_w', 'L0_tok_proj_b', 'L0_attn_w_qkv', 'L0_attn_w_proj', 'L0_attn_b_proj', 'L0_attn_slopes',
        'L0_ffn_router_w', 'L0_ffn_w1', 'L0_ffn_b1', 'L0_ffn_w2', 'L0_ffn_b2']
_OUTS = [((128, 256, 64), 'float32')]


def kernel(**inputs):
    import numpy as _np
    import concourse.bacc as _bacc
    from concourse import mybir as _mybir
    from concourse.bass_utils import run_bass_kernel_spmd as _run

    nc = _bacc.Bacc("TRN2", target_bir_lowering=False, num_devices=1)
    arrays, args = {}, []
    for name in _INS:
        a = _np.ascontiguousarray(inputs[name])
        arrays[f"in_{name}_dram"] = a
        args.append(nc.dram_tensor(f"in_{name}_dram", a.shape, _mybir.dt.from_np(a.dtype), kind="ExternalInput").ap())
    for i, (shape, dtype) in enumerate(_OUTS):
        dt = _mybir.dt.from_np(_np.dtype(dtype))
        args.append(nc.dram_tensor(f"out_{i}_dram", shape, dt, kind="ExternalOutput").ap())
    vit_tower_kernel(nc, *args)
    r = _run(nc, [arrays], core_ids=[0])
    return r.results[0]["out_0_dram"]
```

```python
from contextlib import ExitStack

import concourse.bass as bass
from concourse import mybir

ALU = mybir.AluOpType
ACT = mybir.ActivationFunctionType
AX = mybir.AxisListType.X
F32 = mybir.dt.float32
I32 = mybir.dt.int32


def vit_tower_kernel(nc, x, ln_q_w, ln_q_b, Wq, ln_kv_w, ln_kv_b, Wkv, proj_w, proj_b,
                     w_qkv, w_proj, b_proj, slopes, router_w, w1, b1, w2, b2, out):
    P = 128
    B, C, HH, WW = x.shape
    ST = 4
    N = ST * ST
    PX = HH * WW // 2
    HEADS = slopes.shape[0]
    D = C // HEADS
    E = router_w.shape[0]
    SL = 2 * HEADS
    UNITS = B
    TOK_SCALE = float(C) ** -0.5
    ATT_SCALE = float(D) ** -0.5
    EPS = 1e-5
    GN = 4
    NG = N // GN
    NS = N // 2
    assert (C, D, N, P) == (64, 8, 16, 128) and B % 2 == 0

    def done(i, s, lag, per, plus=0):
        if isinstance(i, int):
            return max(0, max(0, min(UNITS, 2 * i + s - lag + 1)) * per + plus)
        return i * (2 * per) + (s - lag + 1) * per + plus

    def there(i, s, lag):
        return not isinstance(i, int) or 0 <= 2 * i + s - lag < UNITS

    def pairs(i, back, per=1):
        if isinstance(i, int):
            return max(0, min(UNITS // 2, i + back)) * per
        return i * per + back * per

    def floor0(n):
        return max(0, n) if isinstance(n, int) else n

    def chain(eng, sem, base):
        n = [0]

        def link(ins):
            n[0] += 1
            ins.then_inc(sem, 1)
            eng.wait_ge(sem, base + n[0])
        return link, n

    def units(eng, step):
        step(-1, 1)
        for i in range(4):
            step(i, 0)
            step(i, 1)
        with eng.Fori(4, UNITS // 2 - 1) as i:
            step(i, 0)
            step(i, 1)
        for i in range(UNITS // 2 - 1, UNITS // 2 + 3):
            step(i, 0)
            step(i, 1)

    with ExitStack() as ctx:
        def sb(name, shape, dt=F32):
            return ctx.enter_context(nc.sbuf_tensor(name, shape, dt))

        def sem(name):
            return ctx.enter_context(nc.semaphore(name))

        ps = ctx.enter_context(nc.psum_tensor("ps", [P, 8, 512], F32))
        psf = ps[:].rearrange("p b c -> p (b c)")
        KB = [ps[:, 0, :], ps[:, 1, :]]
        CVB = [ps[:, 2, :], ps[:, 3, :]]
        SCB = [ps[:, 4, :], ps[:, 5, :]]
        B6 = ps[:, 6, :]
        B7 = ps[:, 7, :]

        ident = sb("ident", [P, P])
        ident2 = sb("ident2", [P, P])
        ones = sb("ones", [P, P])
        blockmask = sb("blockmask", [P, P])
        headmask = sb("headmask", [P, SL])
        w_ckv = sb("w_ckv", [P, 3 * P])
        w_q_id = sb("w_q_id", [P, 2 * P])
        w_pj = sb("w_pj", [P, P])
        w_aq = sb("w_aq", [P, P])
        w_avki = sb("w_avki", [P, 3 * P])
        w_ap = sb("w_ap", [P, P])
        bk_row = sb("bk_row", [P, P])
        bq_row = sb("bq_row", [P, P])
        bp_row = sb("bp_row", [P, P])
        bv_col = sb("bv_col", [P, 1])
        pb_col = sb("pb_col", [P, 1])
        decay = sb("decay", [P, HEADS, P])
        kdec = sb("kdec", [P, HEADS])
        qdec = sb("qdec", [P, P])
        h1 = sb("h1", [P, UNITS, P])

        with ExitStack() as early:
            def sb1(name, shape, dt=F32):
                return early.enter_context(nc.sbuf_tensor(name, shape, dt))

            sm = sb1("sm", [P, SL * P])
            cat = sm[:, 0:4 * P].rearrange("p (j c) -> p j c", j=4)
            scr = sm[:, 4 * P:8 * P].rearrange("p (j c) -> p j c", j=4)
            rows = sm[:, 8 * P:10 * P].rearrange("p (j c) -> p j c", j=4)
            lnb = sm[:, 10 * P:12 * P].rearrange("p (j c) -> p j c", j=4)
            diff = sm[:, 12 * P:13 * P]
            tril = sm[:, 13 * P:14 * P]
            qd_tok = sm[:, 14 * P:15 * P]
            col = sb1("col", [P, 8])
            diffi = sb1("diffi", [P, P], I32)
            posi = sb1("posi", [P, 1], I32)
            pos = sb1("pos", [P, 3])
            slb = sb1("slb", [P, 8])
            nsl = sb1("nsl", [P, 8])
            bprow64 = sb1("bprow64", [P, 64])
            xb = sb1("xb", [P, 2, PX])
            sq = sb1("sq", [P, 2, N * P])
            vs = sb1("vs", [P, 2, N * P])
            kq = sb1("kq", [P, N * P])
            pv = sb1("pv", [P, N * P])
            NV = 2 * N + 4
            ssq = sb1("ssq", [P, 2, NV])
            var = sb1("var", [P, NV])
            yrs = sb1("yrs", [P, NV])
            yt = sb1("yt", [P, NV])
            sc = sb1("sc", [P, N * SL])
            ex = sb1("ex", [P, N * SL])
            aw = sb1("aw", [P, N * SL])
            mx = sb1("mx", [P, SL])
            den = sb1("den", [P, SL])
            rden = sb1("rden", [P, SL])
            agg = sb1("agg", [P, P])
            aggn = sb1("aggn", [P, P])
            aggT = sb1("aggT", [P, P])
            rsum = sb1("rsum", [P, P])
            red = sb1("red", [P, P])
            qps = sb1("qps", [P, 2 * P])
            hT = sb1("hT", [P, 2, P])
            qc = sb1("qc", [P, P])
            q2 = sb1("q2", [P, P])
            qq = sb1("qq", [P, 2, P])
            qst = sb1("qst", [P, 2, 2])
            sbias = sb1("sbias", [P, 2, SL])
            qT = sb1("qT", [P, 2, P])
            kT = sb1("kT", [P, 2, P])
            VW = P + D
            vpad = sb1("vpad", [P, 2, SL * VW])
            vpl = sb1("vpl", [P, P])
            kpl = sb1("kpl", [P, P])
            kd = sb1("kd", [P, P])
            qdm = sb1("qdm", [P, P])
            sblk = sb1("sblk", [P, P])
            htok = sb1("htok", [P, 2, P])
            qm = sb1("qm", [P, 2, SL * P])
            oT = sb1("oT", [P, P])
            lt = sb1("lt", [P, P])
            l2 = sb1("l2", [P, P])
            lst = sb1("lst", [P, 2, 2])

            ld_w = sem("ld_w")
            s_zero = sem("s_zero")
            s_pool0 = sem("s_pool0")
            s_set = sem("s_set")
            s_dve0 = sem("s_dve0")
            s_act0 = sem("s_act0")
            s_pe0 = sem("s_pe0")
            x_in = [sem("x_in0"), sem("x_in1")]
            grp = sem("grp")
            kq_done = sem("kq_done")
            cv_done = sem("cv_done")
            tree_ch = sem("tree_ch")
            ssq_done = sem("ssq_done")
            newt_ch = sem("newt_ch")
            dred_done = sem("dred_done")
            soft_ch = sem("soft_ch")
            s3_done = sem("s3_done")
            ex_done = sem("ex_done")
            aw_done = sem("aw_done")
            pv_done = sem("pv_done")
            agg_ch = sem("agg_ch")
            agg_done = sem("agg_done")
            agT_pe = sem("agT_pe")
            agT_ev = sem("agT_ev")
            pj_done = sem("pj_done")
            hT_done = sem("hT_done")
            xs_ch = sem("xs_ch")
            xs_done = sem("xs_done")
            rcp_done = sem("rcp_done")
            qp_pe = sem("qp_pe")
            qp_ev = sem("qp_ev")
            q_ch = sem("q_ch")
            qp_done = sem("qp_done")
            qk_pe = sem("qk_pe")
            qk_ev = sem("qk_ev")
            vk_pe = sem("vk_pe")
            vk_ev = sem("vk_ev")
            st_ev = sem("st_ev")
            kd_done = sem("kd_done")
            s_pe = sem("s_pe")
            sb_done = sem("sb_done")
            qd_done = sem("qd_done")
            qm_done = sem("qm_done")
            sc_done = sem("sc_done")
            mask_done = sem("mask_done")
            o_done = sem("o_done")
            oT_done = sem("oT_done")
            pr_done = sem("pr_done")
            lt_done = sem("lt_done")
            ln_ch = sem("ln_ch")
            h1_done = sem("h1_done")

            LOADS = 24
            block = early.enter_context(nc.Block())

            xr = x.rearrange("n c (s a b) w -> (n c) s a b w", s=2, b=ST)

            def row(ap, n):
                return ap.unsqueeze(0).to_broadcast([P, n])

            @block.sync
            def _(sp):
                sp.wait_ge(s_zero, 8)
                todo = [
                    (rows[0:64, 0, :], Wq), (rows[64:128, 0, :], Wq),
                    (rows[0:64, 1, :], Wkv[0:64, :]), (rows[64:128, 1, :], Wkv[0:64, :]),
                    (rows[0:64, 2, :], Wkv[64:128, :]), (rows[64:128, 2, :], Wkv[64:128, :]),
                    (rows[0:64, 3, :], proj_w), (rows[64:128, 3, :], proj_w),
                    (lnb[:, 0, :], row(ln_q_w, 64)), (lnb[:, 1, :], row(ln_q_b, 64)),
                    (lnb[:, 2, :], row(ln_kv_w, 64)), (lnb[:, 3, :], row(ln_kv_b, 64)),
                    (bprow64[:], row(b_proj, 64)), (slb[:], row(slopes, 8)),
                ]
                for m in range(2):
                    r = slice(64 * m, 64 * m + 64)
                    todo += [
                        (pb_col[r, :], proj_b.unsqueeze(1)),
                        (w_aq[r, 64 * m:64 * m + 64], w_qkv[:, 0:64]),
                        (w_avki[r, 64 * m:64 * m + 64], w_qkv[:, 128:192]),
                        (w_avki[r, P + 64 * m:P + 64 * m + 64], w_qkv[:, 64:128]),
                        (w_ap[r, 64 * m:64 * m + 64], w_proj),
                    ]
                for dst, src in todo:
                    sp.dma_start(dst, src).then_inc(ld_w, 16)
                assert len(todo) == LOADS

                def load(i, s):
                    sp.wait_ge(grp, done(i, s, 2, NS))
                    for b in range(ST):
                        sp.dma_start(xb[:, s, b * PX // ST:(b + 1) * PX // ST].rearrange("p (a w) -> p a w", w=WW),
                                     xr[bass.ds(i * P, P), s, :, b, :]).then_inc(x_in[s], 16)
                load(0, 0)
                load(0, 1)
                with sp.Fori(1, UNITS // 2) as i:
                    load(i, 0)
                    load(i, 1)

            @block.tensor
            def _(pe):
                pe.wait_ge(s_dve0, 1)
                for j in range(4):
                    nc.tensor.transpose(ps[:, 0, j * P:(j + 1) * P], cat[:, j, :], ident[:])
                for j in range(2):
                    nc.tensor.matmul(ps[:, 1, j * P:(j + 1) * P], ones[:], scr[:, j, :], start=True, stop=True)
                pe.wait_ge(s_act0, 1)
                nc.tensor.transpose(ps[:, 1, 2 * P:3 * P], qd_tok[:], ident[:]).then_inc(s_pe0, 1)
                pe.wait_ge(s_dve0, 2)

                def step(i, s):
                    o = 1 - s
                    xv = xb[:, s, :].rearrange("p (b k d) -> p b d k", b=ST, d=ST)

                    def two_pixels(j):
                        if not there(i, s, 0):
                            return
                        g = j // 2
                        if j == 0:
                            pe.wait_ge(x_in[s], (i + 1) * 16 * ST)
                            pe.wait_ge(qp_done, done(i, s, 0, 1))
                        if j % 2 == 0:
                            pe.wait_ge(kq_done, done(i, s, 1, NG, g - 1))
                        pe.wait_ge(cv_done, done(i, s, 1, 2 * NS, 2 * (j - 1)))
                        for n in (2 * j, 2 * j + 1):
                            nc.tensor.matmul(KB[g % 2][:, (n % GN) * P:(n % GN + 1) * P], xv[:, n // ST, n % ST],
                                             w_ckv[:, 2 * P:3 * P], start=True, stop=True)
                        for n in (2 * j, 2 * j + 1):
                            mm = nc.tensor.matmul(CVB[j % 2][:, (n % 2) * 2 * P:(n % 2 + 1) * 2 * P],
                                                  xv[:, n // ST, n % ST], w_ckv[:, 0:2 * P], start=True, stop=True)
                        mm.then_inc(grp, 1)

                    def queries():
                        if there(i, s, -1):
                            pe.wait_ge(xs_done, done(i, s, -1, 1))
                            pe.wait_ge(hT_done, done(i, s, 3, 1))
                            pe.wait_ge(sb_done, pairs(i, -1))
                            nc.tensor.matmul(B6[:, 0:2 * P], red[:], w_q_id[:], start=True,
                                             stop=True).then_inc(qp_pe, 1)

                    def attn_qk():
                        if there(i, s, 3):
                            pe.wait_ge(qp_ev, done(i, s, -1, 1))
                            pe.wait_ge(hT_done, done(i, s, 3, 1))
                            nc.tensor.matmul(B6[:, 0:P], w_aq[:], hT[:, o, :], start=True, stop=True)
                            nc.tensor.matmul(B6[:, P:2 * P], w_avki[:, P:2 * P], hT[:, o, :], start=True,
                                             stop=True).then_inc(qk_pe, 1)

                    def attn_vk():
                        if there(i, s, 3):
                            pe.wait_ge(qk_ev, done(i, s, 3, 2))
                            nc.tensor.matmul(B6[:, 0:3 * P], hT[:, o, :], w_avki[:], start=True,
                                             stop=True).then_inc(vk_pe, 1)

                    def scores(r):
                        if there(i, s, 4):
                            pe.wait_ge(qm_done, done(i, s, 4, 1))
                            pe.wait_ge(qk_ev, done(i, s, 4, 2))
                            pe.wait_ge(mask_done, done(i, s, 5, 4, r - 1))
                            nc.tensor.matmul(SCB[r % 2], kT[:, s, :], qm[:, s, r * 512:(r + 1) * 512],
                                             start=True, stop=True).then_inc(sc_done, 1)

                    def attend(r):
                        if not there(i, s, 4):
                            return
                        if r == 0:
                            pe.wait_ge(lt_done, done(i, s, 5, 1))
                            pe.wait_ge(vk_ev, done(i, s, 4, 2))
                        pe.wait_ge(mask_done, done(i, s, 5, 4, r + 1))
                        for j in range(4 * r, 4 * r + 4):
                            mm = nc.tensor.matmul(B7[:, 0:P], vpad[:, s, j * P:(j + 1) * P],
                                                  sm[:, j * P:(j + 1) * P], start=(j == 0),
                                                  stop=(j == SL - 1 and s == 0))
                        if r == 3:
                            if s == 1:
                                pe.wait_ge(sb_done, pairs(i, -1))
                                pe.wait_ge(qd_done, pairs(i, -1))
                                mm = nc.tensor.matmul(B7[:, 0:P], sblk[:], qdm[:], start=False, stop=True)
                            mm.then_inc(o_done, 1)

                    two_pixels(0)
                    scores(0)
                    queries()
                    two_pixels(1)
                    scores(1)
                    two_pixels(2)
                    attend(0)
                    attn_qk()
                    two_pixels(3)
                    scores(2)
                    attend(1)
                    two_pixels(4)
                    attn_vk()
                    scores(3)
                    two_pixels(5)
                    attend(2)
                    two_pixels(6)
                    attend(3)
                    if there(i, s, 2):
                        pe.wait_ge(agg_done, done(i, s, 2, 1))
                        pe.wait_ge(qp_ev, done(i, s, -1, 1))
                        pe.wait_ge(vk_ev, done(i, s, 3, 2))
                        if s == 1:
                            pe.wait_ge(st_ev, pairs(i, 0, 2))
                        nc.tensor.transpose(B6[:, 0:P], aggn[:], ident[:]).then_inc(agT_pe, 1)
                    two_pixels(7)
                    if there(i, s, 3) and s == 1:
                        pe.wait_ge(kd_done, pairs(i, 0))
                        pe.wait_ge(agT_ev, done(i, s, 2, 1))
                        pe.wait_ge(vk_ev, done(i, s, 3, 2))
                        nc.tensor.matmul(B6[:, 3 * P:4 * P], kd[:], vpl[:], start=True, stop=True).then_inc(s_pe, 1)
                    if there(i, s, 2):
                        pe.wait_ge(agT_ev, done(i, s, 2, 1))
                        nc.tensor.matmul(B6[:, P:2 * P], w_pj[:], aggT[:], start=True, stop=True).then_inc(pj_done, 1)
                    if there(i, s, 4):
                        pe.wait_ge(oT_done, done(i, s, 4, 1))
                        nc.tensor.matmul(B7[:, P:2 * P], oT[:], w_ap[:], start=True, stop=True).then_inc(pr_done, 1)
                units(pe, step)

            @block.scalar
            def _(act):
                act.wait_ge(s_dve0, 1)
                for h in range(HEADS):
                    nc.scalar.activation(decay[:, h, :], diff[:], ACT.Exp, scale=nsl[:, h:h + 1])
                nc.scalar.activation(kdec[:], nsl[:], ACT.Exp, scale=pos[:, 1:2])
                nc.scalar.activation(qd_tok[:], scr[:, 2, :], ACT.Exp, scale=pos[:, 0:1]).then_inc(s_act0, 1)
                act.wait_ge(s_dve0, 2)

                def step(i, s):
                    o = 1 - s

                    def pixels_values(j):
                        if not there(i, s, 0):
                            return
                        if j == 0:
                            act.wait_ge(ssq_done, done(i, s, 2, 2))
                            act.wait_ge(pv_done, done(i, s, 2, 1))
                        act.wait_ge(grp, done(i, s, 1, NS, j + 1))
                        cvw = CVB[j % 2].rearrange("p (n c) -> p n c", c=2 * P)
                        at = slice(2 * j * P, (2 * j + 2) * P)
                        nc.scalar.activation(sq[:, s, at].rearrange("p (n c) -> p n c", c=P),
                                             cvw[:, :, 0:P], ACT.Square).then_inc(cv_done, 1)
                        nc.scalar.activation(vs[:, s, at].rearrange("p (n c) -> p n c", c=P),
                                             cvw[:, :, P:2 * P], ACT.Copy).then_inc(cv_done, 1)

                    pixels_values(0)
                    if there(i, s, -1):
                        act.wait_ge(qp_pe, done(i, s, -1, 1))
                        act.wait_ge(qp_done, done(i, s, 0, 1))
                        nc.scalar.activation(qps[:], B6[:, 0:2 * P], ACT.Copy).then_inc(qp_ev, 1)
                        act.wait_ge(xs_done, done(i, s, -1, 1))
                        nc.scalar.activation(h1[:, bass.ds(2 * i + s + 1, 1), :], red[:].unsqueeze(1),
                                             ACT.Copy).then_inc(rcp_done, 1)
                    pixels_values(1)
                    pixels_values(2)
                    if there(i, s, 3):
                        act.wait_ge(qk_pe, done(i, s, 3, 1))
                        act.wait_ge(sc_done, done(i, s, 5, 4))
                        act.wait_ge(qm_done, done(i, s, 5, 1))
                        act.wait_ge(o_done, done(i, s, 5, 1))
                        nc.scalar.activation(qT[:, o, :], B6[:, 0:P], ACT.Copy, scale=ATT_SCALE).then_inc(qk_ev, 1)
                        nc.scalar.activation(kT[:, o, :], B6[:, P:2 * P], ACT.Copy).then_inc(qk_ev, 1)
                    pixels_values(3)
                    pixels_values(4)
                    if there(i, s, 3):
                        act.wait_ge(vk_pe, done(i, s, 3, 1))
                        act.wait_ge(lt_done, done(i, s, 5, 1))
                        nc.scalar.activation(
                            vpad[:, o, :].rearrange("p (j w) -> p j w", w=VW)[:, :, 0:D],
                            B6[:, 0:P].rearrange("p (j d) -> p j d", d=D), ACT.Copy).then_inc(vk_ev, 1)
                        if s == 1:
                            act.wait_ge(s_pe, pairs(i, -1))
                            act.wait_ge(kd_done, pairs(i, -1))
                            nc.scalar.activation(vpl[:], B6[:, 0:P], ACT.Copy).then_inc(st_ev, 1)
                            nc.scalar.activation(kpl[:], B6[:, P:2 * P], ACT.Copy).then_inc(st_ev, 1)
                        nc.scalar.activation(htok[:, o, :], B6[:, 2 * P:3 * P], ACT.Copy).then_inc(vk_ev, 1)
                    pixels_values(5)
                    if there(i, s, 1):
                        act.wait_ge(s3_done, done(i, s, 1, 1))
                        nc.scalar.activation(ex[:], sc[:], ACT.Exp, scale=TOK_SCALE).then_inc(ex_done, 1)
                    pixels_values(6)
                    if there(i, s, 2):
                        act.wait_ge(agT_pe, done(i, s, 2, 1))
                        act.wait_ge(pj_done, done(i, s, 3, 1))
                        nc.scalar.activation(aggT[:], B6[:, 0:P], ACT.Identity, bias=bv_col[:, 0:1]).then_inc(agT_ev, 1)
                    pixels_values(7)
                    if there(i, s, 4):
                        act.wait_ge(o_done, done(i, s, 4, 1))
                        act.wait_ge(pr_done, done(i, s, 5, 1))
                        nc.scalar.activation(oT[:], B7[:, 0:P], ACT.Copy).then_inc(oT_done, 1)
                units(act, step)

            @block.gpsimd
            def _(pool):
                for t in (w_aq, w_ap, w_avki, vpad, ident, blockmask):
                    nc.gpsimd.memset(t[:], 0.0).then_inc(s_zero, 1)
                nc.gpsimd.memset(ones[:], 1.0).then_inc(s_zero, 1)
                nc.gpsimd.memset(headmask[:], 1.0).then_inc(s_zero, 1)
                nc.gpsimd.iota(diffi[:], pattern=[[1, P]], base=0, channel_multiplier=-1).then_inc(s_pool0, 1)
                nc.gpsimd.iota(posi[:], pattern=[[0, 1]], base=0, channel_multiplier=1).then_inc(s_pool0, 1)
                link, n = chain(pool, s_pool0, 2)
                pool.wait_ge(s_pool0, 2)
                pool.wait_ge(s_zero, 8)
                link(nc.gpsimd.affine_select(out=ident[:], in_=ident[:], compare_op=ALU.not_equal, fill=1.0, base=0,
                                             pattern=[[-1, P]], channel_multiplier=1))
                for m in range(2):
                    link(nc.gpsimd.memset(blockmask[64 * m:64 * m + 64, 64 * m:64 * m + 64], 1.0))
                for base, pattern, step_p in ((0, [[-D, SL]], 1), (D - 1, [[D, SL]], -1)):
                    link(nc.gpsimd.affine_select(out=headmask[:], in_=headmask[:], compare_op=ALU.is_ge, fill=0.0,
                                                 base=base, pattern=pattern, channel_multiplier=step_p))

                def step(i, s):
                    o = 1 - s

                    def squares(half):
                        if not there(i, s, 0):
                            return
                        link, n = chain(pool, tree_ch, done(i, s, 1, 10) + 5 * half)
                        pool.wait_ge(cv_done, done(i, s, 1, 2 * NS, NS * (half + 1)))
                        if half == 0:
                            pool.wait_ge(aw_done, done(i, s, 2, 1))
                        v = sq[:, s, half * N * C:(half + 1) * N * C].rearrange("p (n c) -> p n c", c=C)
                        w = C // 2
                        while w > 1:
                            link(nc.gpsimd.tensor_tensor(v[:, :, 0:w], v[:, :, 0:w], v[:, :, w:2 * w], ALU.add))
                            w //= 2
                        nc.gpsimd.tensor_tensor(ssq[:, s, half * N:(half + 1) * N].unsqueeze(2), v[:, :, 0:1],
                                                v[:, :, 1:2], ALU.add).then_inc(ssq_done, 1)

                    if there(i, s, 3):
                        pool.wait_ge(qk_ev, done(i, s, 3, 2))
                        pool.wait_ge(sc_done, done(i, s, 5, 4))
                        nc.gpsimd.tensor_tensor(
                            qm[:, o, :].rearrange("p (j c) -> p j c", c=P),
                            qT[:, o, :].unsqueeze(1).to_broadcast([P, SL, P]),
                            headmask[:].unsqueeze(2).to_broadcast([P, SL, P]), ALU.mult).then_inc(qm_done, 1)
                    squares(0)
                    if there(i, s, 1):
                        pool.wait_ge(aw_done, done(i, s, 1, 1))
                        nc.gpsimd.tensor_tensor(
                            pv[:].rearrange("p (k d) -> p k d", d=D),
                            vs[:, o, :].rearrange("p (k d) -> p k d", d=D),
                            aw[:].unsqueeze(2).to_broadcast([P, N * SL, D]), ALU.mult).then_inc(pv_done, 1)
                    squares(1)
                units(pool, step)

            @block.vector
            def _(dve):
                dve.wait_ge(s_pool0, 7)
                dve.wait_ge(ld_w, 16 * LOADS)
                link, n = chain(dve, s_set, 0)
                V = nc.vector
                link(V.memset(ssq[:], 1.0))
                link(V.tensor_copy(diff[:], diffi[:]))
                link(V.tensor_scalar(tril[:], diff[:], 0.0, None, ALU.is_ge))
                link(V.tensor_scalar(diff[:], diff[:], 0.0, None, ALU.max))
                link(V.tensor_copy(pos[:, 0:1], posi[:]))
                link(V.tensor_scalar(pos[:, 1:2], pos[:, 0:1], -1.0, float(P), ALU.mult, ALU.add))
                link(V.tensor_scalar(nsl[:], slb[:], -1.0, None, ALU.mult))
                for m in range(2):
                    link(V.tensor_copy(scr[:, 2, m * C:(m + 1) * C].rearrange("p (h d) -> p h d", d=D),
                                       nsl[:].unsqueeze(2).to_broadcast([P, HEADS, D])))
                    link(V.tensor_copy(bp_row[:, m * C:(m + 1) * C], bprow64[:]))
                for j, b_at, dst in ((0, 1, col[:, 0:1]), (1, 3, col[:, 1:2]), (2, 3, bv_col[:])):
                    link(V.tensor_tensor(scr[:, 3, 0:C], rows[:, j, :], lnb[:, b_at, :], ALU.mult))
                    link(V.tensor_reduce(dst, scr[:, 3, 0:C], AX, ALU.add))
                for j, g_at in ((0, 0), (1, 2), (2, 2)):
                    link(V.tensor_tensor(rows[:, j, :], rows[:, j, :], lnb[:, g_at, :], ALU.mult))
                    link(V.tensor_reduce(col[:, 2:3], rows[:, j, :], AX, ALU.add))
                    link(V.tensor_scalar(col[:, 3:4], col[:, 2:3], -1.0 / C, None, ALU.mult))
                    link(V.tensor_scalar(rows[:, j, :], rows[:, j, :], col[:, 3:4], None, ALU.add))
                for j in range(4):
                    for m in range(2):
                        link(V.tensor_copy(cat[:, j, m * C:(m + 1) * C], rows[:, j, :]))
                link(V.tensor_scalar(scr[:, 0, :], ident[:], col[:, 0:1], None, ALU.mult))
                link(V.tensor_scalar(scr[:, 1, :], ident[:], col[:, 1:2], None, ALU.mult))
                link(V.tensor_scalar(ident2[:], ident[:], 2.0, None, ALU.mult))
                link(V.scalar_tensor_tensor(w_ckv[:, 0:P], blockmask[:], -1.0 / C, ident[:], ALU.mult, ALU.add))
                link(V.tensor_copy(w_q_id[:, P:2 * P], ident[:]))
                V.tensor_copy(w_avki[:, 2 * P:3 * P], ident[:]).then_inc(s_dve0, 1)
                dve.wait_ge(s_pe0, 1)
                for j, dst in ((0, w_q_id[:, 0:P]), (1, w_ckv[:, 2 * P:3 * P]), (2, w_ckv[:, P:2 * P]), (3, w_pj[:])):
                    link(V.tensor_tensor(dst, ps[:, 0, j * P:(j + 1) * P], blockmask[:], ALU.mult))
                link(V.tensor_copy(bq_row[:], ps[:, 1, 0:P]))
                link(V.tensor_copy(bk_row[:], ps[:, 1, P:2 * P]))
                link(V.tensor_copy(qdec[:], ps[:, 1, 2 * P:3 * P]))
                V.tensor_tensor(decay[:], decay[:], tril[:].unsqueeze(1).to_broadcast([P, HEADS, P]),
                                ALU.mult).then_inc(s_dve0, 1)
                dve.wait_ge(s_dve0, 2)

                def heads(ap):
                    return ap.rearrange("p (m c) -> p m c", c=C)

                def step(i, s):
                    o = 1 - s

                    def keys(g):
                        if there(i, s, 0):
                            dve.wait_ge(grp, done(i, s, 1, NS, 2 * g + 2))
                            V.tensor_tensor(kq[:, g * GN * P:(g + 1) * GN * P].rearrange("p (n c) -> p n c", c=P),
                                            KB[g % 2].rearrange("p (n c) -> p n c", c=P),
                                            qq[:, s, :].unsqueeze(1).to_broadcast([P, GN, P]),
                                            ALU.mult).then_inc(kq_done, 1)

                    def mask(r):
                        if there(i, s, 4):
                            if r == 0:
                                dve.wait_ge(o_done, done(i, s, 5, 1))
                            dve.wait_ge(sc_done, done(i, s, 5, 4, r + 1))
                            V.tensor_tensor(sm[:, r * 512:(r + 1) * 512].rearrange("p (h c) -> p h c", c=P),
                                            SCB[r % 2].rearrange("p (h c) -> p h c", c=P),
                                            decay[:, 4 * (r % 2):4 * (r % 2) + 4, :], ALU.mult).then_inc(mask_done, 1)

                    if there(i, s, 4) and s == 1:
                        dve.wait_ge(o_done, done(i, s, 6, 1))
                        V.tensor_tensor(qdm[:], qT[:, s, :], qdec[:], ALU.mult).then_inc(qd_done, 1)
                    if there(i, s, -1):
                        link, n = chain(dve, xs_ch, done(i, s, 0, 1))
                        dve.wait_ge(x_in[o], 16 * ST * (i + 1 if s == 0 else i + 2))
                        link(V.tensor_reduce(rsum[:], xb[:, o, :].rearrange("p (b k d) -> p k b d", b=ST, d=ST),
                                             mybir.AxisListType.XY, ALU.add))
                        dve.wait_ge(qp_pe, done(i, s, 0, 1))
                        dve.wait_ge(rcp_done, done(i, s, 0, 1))
                        V.tensor_scalar(red[:], rsum[:], 1.0 / N, None, ALU.mult).then_inc(xs_done, 1)
                    if there(i, s, 2):
                        link, n = chain(dve, agg_ch, done(i, s, 3, 1))
                        dve.wait_ge(pv_done, done(i, s, 2, 1))
                        link(V.tensor_reduce(agg[:], pv[:].rearrange("p (n c) -> p c n", c=P), AX, ALU.add))
                        dve.wait_ge(agT_pe, done(i, s, 3, 1))
                        V.tensor_tensor(aggn[:].rearrange("p (j d) -> p j d", d=D),
                                        agg[:].rearrange("p (j d) -> p j d", d=D),
                                        rden[:].unsqueeze(2).to_broadcast([P, SL, D]), ALU.mult).then_inc(agg_done, 1)
                    mask(0)
                    keys(0)
                    mask(1)
                    if there(i, s, 5):
                        link_l, nl = chain(dve, ln_ch, done(i, s, 6, 6))
                        dve.wait_ge(lt_done, done(i, s, 5, 1))
                        link_l(V.tensor_tensor(lt[:], lt[:], bp_row[:], ALU.add))
                        link_l(V.tensor_reduce(lst[:, 0, :], heads(lt[:]), AX, ALU.add))
                        link_l(V.tensor_scalar(lst[:, 1, :], lst[:, 0, :], -1.0 / C, None, ALU.mult))
                        link_l(V.tensor_tensor(heads(lt[:]), heads(lt[:]),
                                               lst[:, 1, :].unsqueeze(2).to_broadcast([P, 2, C]), ALU.add))
                        link_l(V.tensor_tensor(l2[:], lt[:], lt[:], ALU.mult))
                        link_l(V.tensor_reduce(ssq[:, o, 2 * N:2 * N + 2], heads(l2[:]), AX, ALU.add))
                        assert nl[0] == 6
                    if there(i, s, -1):
                        link_q, nq = chain(dve, q_ch, done(i, s, 0, 8))
                        dve.wait_ge(qp_ev, done(i, s, -1, 1))
                        link_q(V.tensor_reduce(qst[:, 0, :], heads(qps[:, P:2 * P]), AX, ALU.add))
                        link_q(V.tensor_scalar(qst[:, 1, :], qst[:, 0, :], -1.0 / C, None, ALU.mult))
                        link_q(V.tensor_tensor(heads(qc[:]), heads(qps[:, P:2 * P]),
                                               qst[:, 1, :].unsqueeze(2).to_broadcast([P, 2, C]), ALU.add))
                        link_q(V.tensor_tensor(q2[:], qc[:], qc[:], ALU.mult))
                        link_q(V.tensor_reduce(ssq[:, o, 2 * N + 2:2 * N + 4], heads(q2[:]), AX, ALU.add))
                    keys(1)
                    mask(2)
                    link, n = chain(dve, newt_ch, (2 * i + s + 1) * 11)
                    dve.wait_ge(ssq_done, done(i, s, 1, 2))
                    link(V.tensor_scalar(var[:], ssq[:, o, :], 1.0 / C, EPS, ALU.mult, ALU.add))
                    link(V.tensor_scalar(yrs[:].bitcast(I32), var[:].bitcast(I32), -0.5, float(0x5f3759df),
                                         ALU.mult, ALU.add))
                    for _ in range(3):
                        link(V.scalar_tensor_tensor(yt[:], yrs[:], -0.5, yrs[:], ALU.mult, ALU.mult))
                        link(V.tensor_tensor(yt[:], yt[:], var[:], ALU.mult))
                        link(V.scalar_tensor_tensor(yrs[:], yt[:], 1.5, yrs[:], ALU.add, ALU.mult))
                    assert n[0] == 11
                    rs_b = yrs[:, 0:2 * N].unsqueeze(2).to_broadcast([P, 2 * N, HEADS])
                    if there(i, s, 1):
                        link, n = chain(dve, soft_ch, done(i, s, 2, 5))
                        dve.wait_ge(dred_done, done(i, s, 1, 1))
                        dve.wait_ge(qp_done, done(i, s, 1, 1))
                        s3 = sc[:].rearrange("p (k h) -> p k h", h=HEADS)
                        sn = sc[:].rearrange("p (n j) -> p n j", j=SL)
                        link(V.tensor_tensor(s3, s3, rs_b, ALU.mult))
                        link(V.tensor_tensor(sn, sn, sbias[:, o, :].unsqueeze(1).to_broadcast([P, N, SL]), ALU.add))
                        link(V.tensor_reduce(mx[:], sc[:].rearrange("p (n j) -> p j n", j=SL), AX, ALU.max))
                        V.tensor_tensor(sn, sn, mx[:].unsqueeze(1).to_broadcast([P, N, SL]),
                                        ALU.subtract).then_inc(s3_done, 1)
                    keys(2)
                    mask(3)
                    if there(i, s, 1):
                        dve.wait_ge(ex_done, done(i, s, 1, 1))
                        V.tensor_tensor(aw[:].rearrange("p (k h) -> p k h", h=HEADS),
                                        ex[:].rearrange("p (k h) -> p k h", h=HEADS), rs_b,
                                        ALU.mult).then_inc(aw_done, 1)
                        link(V.tensor_reduce(den[:], ex[:].rearrange("p (n j) -> p j n", j=SL), AX, ALU.add))
                        link(V.reciprocal(rden[:], den[:]))
                        assert n[0] == 5
                    if there(i, s, 5):
                        V.tensor_tensor(h1[:, bass.ds(2 * i + s - 5, 1), :].rearrange("p u (m c) -> p (u m) c", c=C),
                                        heads(lt[:]), yrs[:, 2 * N:2 * N + 2].unsqueeze(2).to_broadcast([P, 2, C]),
                                        ALU.mult).then_inc(h1_done, 1)
                    if there(i, s, 3) and s == 1:
                        dve.wait_ge(st_ev, pairs(i, 0, 2))
                        dve.wait_ge(s_pe, pairs(i, -1))
                        V.tensor_tensor(kd[:].rearrange("p (m h d) -> p m h d", m=2, d=D),
                                        kpl[:].rearrange("p (m h d) -> p m h d", m=2, d=D),
                                        kdec[:].unsqueeze(1).unsqueeze(3).to_broadcast([P, 2, HEADS, D]),
                                        ALU.mult).then_inc(kd_done, 1)
                    if there(i, s, -1):
                        link_q(V.tensor_tensor(heads(q2[:]), heads(qps[:, 0:P]),
                                               yrs[:, 2 * N + 2:2 * N + 4].unsqueeze(2).to_broadcast([P, 2, C]),
                                               ALU.mult))
                        link_q(V.tensor_tensor(qq[:, o, :], q2[:], bq_row[:], ALU.add))
                        link_q(V.tensor_tensor(qc[:], qq[:, o, :], bk_row[:], ALU.mult))
                        assert nq[0] == 8
                        V.tensor_reduce(sbias[:, o, :], qc[:].rearrange("p (j d) -> p j d", d=D), AX,
                                        ALU.add).then_inc(qp_done, 1)
                    keys(3)
                    if there(i, s, 0):
                        dve.wait_ge(kq_done, done(i, s, 0, NG))
                        V.tensor_reduce(sc[:], kq[:].rearrange("p (k d) -> p k d", d=D), AX,
                                        ALU.add).then_inc(dred_done, 1)
                    if there(i, s, 2):
                        dve.wait_ge(pj_done, done(i, s, 2, 1))
                        dve.wait_ge(vk_pe, done(i, s, 4, 1))
                        dve.wait_ge(rcp_done, done(i, s, 2, 1))
                        V.scalar_tensor_tensor(hT[:, s, :].unsqueeze(1), B6[:, P:2 * P].unsqueeze(1), pb_col[:, 0:1],
                                               h1[:, bass.ds(2 * i + s - 2, 1), :],
                                               ALU.add, ALU.add).then_inc(hT_done, 1)
                    if there(i, s, 3) and s == 1:
                        dve.wait_ge(s_pe, pairs(i, 0))
                        dve.wait_ge(o_done, done(i, s, 4, 1))
                        V.tensor_tensor(sblk[:].rearrange("p (j d) -> p j d", d=D),
                                        B6[:, 3 * P:4 * P].rearrange("p (j d) -> p j d", d=D),
                                        headmask[:].unsqueeze(2).to_broadcast([P, SL, D]),
                                        ALU.mult).then_inc(sb_done, 1)
                    if there(i, s, 4):
                        dve.wait_ge(pr_done, done(i, s, 4, 1))
                        dve.wait_ge(h1_done, done(i, s, 5, 1))
                        V.tensor_tensor(lt[:], B7[:, P:2 * P], htok[:, s, :], ALU.add).then_inc(lt_done, 1)
                units(dve, step)

        G = UNITS // 4
        with ExitStack() as late:
            def sb2(name, shape, dt=F32):
                return late.enter_context(nc.sbuf_tensor(name, shape, dt))

            w1bd = sb2("w1bd", [P, E, P])
            w2bd = sb2("w2bd", [P, E, P])
            rt = sb2("rt", [P, 2 * E])
            b1c = sb2("b1c", [P, E])
            b2v = sb2("b2v", [P, 4, P])
            lg = sb2("lg", [P, 2 * UNITS, E])
            ra = sb2("ra", [P, 2 * UNITS, E])
            rb = sb2("rb", [P, 2 * UNITS, E])
            comb = sb2("comb", [P, 2 * UNITS, E])
            r1 = sb2("r1", [P, 2 * UNITS])
            r2 = sb2("r2", [P, 2 * UNITS])
            rank = sb2("rank", [P, E])
            st = sb2("st", [P, 2, 4 * P])
            tokT = sb2("tokT", [P, 2, 4 * P])
            cb = sb2("cb", [P, 2, P])
            cbT = sb2("cbT", [P, 2, P])
            hid = sb2("hid", [P, 2, E, 4 * P])
            pr = sb2("pr", [P, E, P])
            y = sb2("y", [P, 4 * P])
            y2 = sb2("y2", [P, 4 * P])
            nst = sb2("nst", [P, 8, 8])
            nsi = sb2("nsi", [P, 8], I32)
            outb = sb2("outb", [P, 2, 4 * P])

            ld2 = sem("ld2")
            z2 = sem("z2")
            st_a = sem("st_a")
            tr_a = sem("tr_a")
            tv_a = sem("tv_a")
            lg_pe = sem("lg_pe")
            lg_done = sem("lg_done")
            rt_ch = sem("rt_ch")
            rt_sub = sem("rt_sub")
            rt_exp = sem("rt_exp")
            comb_done = sem("comb_done")
            st_b = sem("st_b")
            tr_b = sem("tr_b")
            tv_b = sem("tv_b")
            up_done = sem("up_done")
            gelu_done = sem("gelu_done")
            dn_done = sem("dn_done")
            x0_done = sem("x0_done")
            pr_read = sem("pr_read")
            x0_read = sem("x0_read")
            y_ch = sem("y_ch")
            y_done = sem("y_done")
            out_done = [sem("out_done0"), sem("out_done1")]

            def gdone(i, s, lag, per):
                if isinstance(i, int):
                    return max(0, min(G, 2 * i + s - lag + 1)) * per
                return i * (2 * per) + (s - lag + 1) * per

            def gthere(i, s, lag):
                return not isinstance(i, int) or 0 <= 2 * i + s - lag < G

            def groups(eng, step):
                for i in (0, 1):
                    step(i, 0)
                    step(i, 1)
                with eng.Fori(2, G // 2 - 1) as i:
                    step(i, 0)
                    step(i, 1)
                step(G // 2 - 1, 0)
                step(G // 2 - 1, 1)
                step(G // 2, 0)

            block2 = late.enter_context(nc.Block())
            LOADS2 = 16

            @block2.gpsimd
            def _(pool):
                for t in (w1bd, w2bd, rt, b2v, cb):
                    nc.gpsimd.memset(t[:], 0.0).then_inc(z2, 1)
                for e in range(E):
                    nc.gpsimd.memset(rank[:, e:e + 1], float(E - e)).then_inc(z2, 1)

            @block2.sync
            def _(sp):
                sp.wait_ge(z2, 5 + E)
                todo = []
                for m in range(2):
                    r = slice(64 * m, 64 * m + 64)
                    todo += [(w1bd[r, :, r], w1.rearrange("e i o -> i e o")),
                             (w2bd[r, :, r], w2.rearrange("e i o -> i e o")),
                             (rt[r, m * E:(m + 1) * E], router_w.rearrange("e c -> c e")),
                             (b1c[r, :], b1.rearrange("e c -> c e"))]
                    todo += [(b2v[k * 2 * E + m * E:k * 2 * E + (m + 1) * E, k, r], b2) for k in range(4)]
                assert len(todo) == LOADS2
                for dst, src in todo:
                    sp.dma_start(dst, src, allow_slow_non_contiguous=True).then_inc(ld2, 16)

                def store(i, s):
                    sp.wait_ge(y_done, gdone(i, s, 0, 1))
                    for a in range(2):
                        for c in range(2):
                            k = 2 * a + c
                            sp.dma_start(out[bass.ds(i * 8 + 4 * s + 2 * a, 2), c * P:(c + 1) * P, :].rearrange(
                                "m p d -> p m d"), outb[:, s, k * P:(k + 1) * P].rearrange(
                                "p (m d) -> p m d", m=2)).then_inc(out_done[s], 16)
                with sp.Fori(0, G // 2) as i:
                    store(i, 0)
                    store(i, 1)
                for s in range(2):
                    sp.wait_ge(out_done[s], G // 2 * 64)

            @block2.tensor
            def _(pe):
                pe.wait_ge(ld2, 16 * LOADS2)

                def logits(i, s):
                    pe.wait_ge(st_a, gdone(i, s, 0, 1))
                    pe.wait_ge(tv_a, gdone(i, s, 2, 1))
                    for k in range(4):
                        mm = nc.tensor.transpose(ps[:, s, k * P:(k + 1) * P], st[:, s, k * P:(k + 1) * P], ident[:])
                    mm.then_inc(tr_a, 1)
                    pe.wait_ge(tv_a, gdone(i, s, 0, 1))
                    pe.wait_ge(lg_done, gdone(i, s, 2, 1))
                    for k in range(4):
                        mm = nc.tensor.matmul(ps[:, 2 + s, k * 2 * E:(k + 1) * 2 * E],
                                              tokT[:, s, k * P:(k + 1) * P], rt[:], start=True, stop=True)
                    mm.then_inc(lg_pe, 1)
                logits(0, 0)
                logits(0, 1)
                with pe.Fori(1, G // 2) as i:
                    logits(i, 0)
                    logits(i, 1)

                def turn(i, s):
                    pe.wait_ge(st_b, gdone(i, s, 0, 2))
                    pe.wait_ge(tv_b, gdone(i, s, 1, 2))
                    for k in range(4):
                        nc.tensor.transpose(ps[:, 0, k * P:(k + 1) * P], st[:, s, k * P:(k + 1) * P], ident[:])
                    nc.tensor.transpose(ps[:, 1, 0:P], cb[:, s, :], ident[:]).then_inc(tr_b, 1)

                def step(i, s):
                    o = 1 - s
                    if gthere(i, s, 0):
                        turn(i, s)
                    for e in range(E):
                        if gthere(i, s, 0):
                            if e == 0:
                                pe.wait_ge(tv_b, gdone(i, s, 0, 2))
                            pe.wait_ge(gelu_done, floor0(gdone(i, s, 1, E) + e - 1))
                            nc.tensor.matmul(ps[:, 2 + e % 2, :], w1bd[:, e, :], tokT[:, s, :], start=True,
                                             stop=True).then_inc(up_done, 1)
                        if gthere(i, s, 1):
                            k, f = e // 2, e % 2
                            if e == 0:
                                pe.wait_ge(gelu_done, gdone(i, s, 1, E))
                            pe.wait_ge(pr_read, floor0(gdone(i, s, 2, 8) + e - 1))
                            for q in range(4):
                                mm = nc.tensor.matmul(ps[:, 4 + f, q * P:(q + 1) * P],
                                                      hid[:, o, 4 * f + q, k * P:(k + 1) * P],
                                                      w2bd[:, 4 * f + q, :], start=True, stop=True)
                            mm.then_inc(dn_done, 1)
                            if f == 1:
                                pe.wait_ge(x0_read, floor0(gdone(i, s, 2, 4) + k - 1))
                                nc.tensor.matmul(ps[:, 6 + k % 2, 0:P], cbT[:, o, :], b2v[:, k, :],
                                                 start=True, stop=False)
                                nc.tensor.matmul(ps[:, 6 + k % 2, 0:P], tokT[:, o, k * P:(k + 1) * P], ident2[:],
                                                 start=False, stop=True).then_inc(x0_done, 1)
                groups(pe, step)

            @block2.scalar
            def _(act):
                act.wait_ge(z2, 5 + E)

                def logits(i, s):
                    act.wait_ge(tr_a, gdone(i, s, 2, 1))
                    nc.scalar.activation(st[:, s, :].rearrange("p (k c) -> p k c", c=P),
                                         h1[:, bass.ds(i * 8 + 4 * s, 4), :], ACT.Copy).then_inc(st_a, 1)

                def logits_out(i, s):
                    act.wait_ge(tr_a, gdone(i, s, 0, 1))
                    act.wait_ge(lg_pe, gdone(i, s, 2, 1))
                    nc.scalar.activation(tokT[:, s, :], ps[:, s, :], ACT.Copy).then_inc(tv_a, 1)
                    act.wait_ge(lg_pe, gdone(i, s, 0, 1))
                    nc.scalar.activation(lg[:, bass.ds(i * 16 + 8 * s, 8), :],
                                         ps[:, 2 + s, 0:8 * E].rearrange("p (t e) -> p t e", e=E),
                                         ACT.Copy).then_inc(lg_done, 1)
                logits(0, 0)
                logits(0, 1)
                for s in range(2):
                    logits_out(0, s)
                    logits(1, s)
                with act.Fori(1, G // 2 - 1) as i:
                    for s in range(2):
                        logits_out(i, s)
                        logits(i + 1, s)
                logits_out(G // 2 - 1, 0)
                logits_out(G // 2 - 1, 1)
                act.wait_ge(rt_sub, 1)
                nc.scalar.activation(lg[:], lg[:], ACT.Exp).then_inc(rt_exp, 1)

                def stage(i, s):
                    if s == 0 and isinstance(i, int) and i == 0:
                        act.wait_ge(comb_done, 1)
                    act.wait_ge(tr_b, gdone(i, s, 2, 1))
                    nc.scalar.activation(st[:, s, :].rearrange("p (k c) -> p k c", c=P),
                                         h1[:, bass.ds(i * 8 + 4 * s, 4), :], ACT.Copy).then_inc(st_b, 1)
                    act.wait_ge(pr_read, gdone(i, s, 2, 8))
                    nc.scalar.activation(cb[:, s, 0:8 * E].rearrange("p (t e) -> p t e", e=E),
                                         comb[:, bass.ds(i * 16 + 8 * s, 8), :], ACT.Copy).then_inc(st_b, 1)

                def step(i, s):
                    if gthere(i, s, 0):
                        stage(i, s)
                        act.wait_ge(tr_b, gdone(i, s, 0, 1))
                        act.wait_ge(x0_done, gdone(i, s, 2, 4))
                        nc.scalar.activation(tokT[:, s, :], ps[:, 0, :], ACT.Copy).then_inc(tv_b, 1)
                        nc.scalar.activation(cbT[:, s, :], ps[:, 1, 0:P], ACT.Copy).then_inc(tv_b, 1)
                        act.wait_ge(dn_done, gdone(i, s, 2, 8))
                        for e in range(E):
                            act.wait_ge(up_done, floor0(gdone(i, s, 0, E) - E + 1 + e))
                            nc.scalar.activation(hid[:, s, e, :], ps[:, 2 + e % 2, :], ACT.Gelu,
                                                 bias=b1c[:, e:e + 1]).then_inc(gelu_done, 1)
                groups(act, step)

            @block2.vector
            def _(dve):
                V = nc.vector
                dve.wait_ge(z2, 5 + E)
                dve.wait_ge(lg_done, G)
                T = 2 * UNITS
                link, n = chain(dve, rt_ch, 0)

                def over_e(ap):
                    return ap.unsqueeze(2).to_broadcast([P, T, E])

                rank_b = rank[:].unsqueeze(1).to_broadcast([P, T, E])
                link(V.tensor_reduce(r1[:], lg[:], AX, ALU.max))
                V.tensor_tensor(lg[:], lg[:], over_e(r1[:]), ALU.subtract).then_inc(rt_sub, 1)
                dve.wait_ge(rt_exp, 1)
                link(V.tensor_reduce(r1[:], lg[:], AX, ALU.add))
                link(V.reciprocal(r2[:], r1[:]))
                link(V.tensor_tensor(lg[:], lg[:], over_e(r2[:]), ALU.mult))

                def first_largest(src, hot):
                    link(V.tensor_reduce(r1[:], src, AX, ALU.max))
                    link(V.tensor_tensor(hot, src, over_e(r1[:]), ALU.is_equal))
                    link(V.tensor_tensor(hot, hot, rank_b, ALU.mult))
                    link(V.tensor_reduce(r2[:], hot, AX, ALU.max))
                    link(V.tensor_tensor(hot, hot, over_e(r2[:]), ALU.is_equal))
                first_largest(lg[:], ra[:])
                link(V.scalar_tensor_tensor(comb[:], ra[:], -2.0, lg[:], ALU.mult, ALU.add))
                first_largest(comb[:], rb[:])
                link(V.tensor_tensor(ra[:], ra[:], rb[:], ALU.add))
                link(V.tensor_tensor(lg[:], lg[:], ra[:], ALU.mult))
                link(V.tensor_reduce(r1[:], lg[:], AX, ALU.add))
                link(V.tensor_scalar(r1[:], r1[:], 1e-12, None, ALU.max))
                link(V.reciprocal(r2[:], r1[:]))
                V.tensor_tensor(comb[:], lg[:], over_e(r2[:]), ALU.mult).then_inc(comb_done, 1)

                def per_token(ap):
                    return ap.rearrange("p (t c) -> p t c", c=C)

                def step(i, s):
                    o = 1 - s
                    if not gthere(i, s, 1):
                        return
                    YCH = 4 + 6 + 2 + 16
                    link, n = chain(dve, y_ch, gdone(i, s, 2, YCH))
                    dve.wait_ge(st_b, gdone(i, s, 1, 2))
                    for k in range(4):
                        for f in range(2):
                            j = 2 * k + f
                            dve.wait_ge(dn_done, floor0(gdone(i, s, 1, 8) - 7 + j))
                            wv = cb[:, o, k * 2 * E:(k + 1) * 2 * E].rearrange("p (m e) -> p e m", e=E)
                            ins = V.tensor_tensor(
                                pr[:, 4 * f:4 * f + 4, :].rearrange("p e (m c) -> p e m c", c=C),
                                ps[:, 4 + f, :].rearrange("p (e m c) -> p e m c", e=4, c=C),
                                wv[:, 4 * f:4 * f + 4, :].unsqueeze(3).to_broadcast([P, 4, 2, C]), ALU.mult)
                            ins.then_inc(pr_read, 1)
                        dve.wait_ge(pr_read, floor0(gdone(i, s, 1, 8) - 6 + 2 * k))
                        link(V.tensor_reduce(y[:, k * P:(k + 1) * P], pr[:].rearrange("p e c -> p c e"), AX, ALU.add))
                        dve.wait_ge(x0_done, floor0(gdone(i, s, 1, 4) - 3 + k))
                        ins = V.tensor_tensor(y[:, k * P:(k + 1) * P], ps[:, 6 + k % 2, 0:P],
                                              y[:, k * P:(k + 1) * P], ALU.add)
                        ins.then_inc(x0_read, 1)
                        dve.wait_ge(x0_read, floor0(gdone(i, s, 1, 4) - 3 + k))
                    v, t, yy = nst[:, 2, :], nst[:, 3, :], nst[:, 4, :]
                    link(V.tensor_reduce(nst[:, 0, :], per_token(y[:]), AX, ALU.add))
                    link(V.tensor_scalar(nst[:, 1, :], nst[:, 0, :], -1.0 / C, None, ALU.mult))
                    link(V.tensor_tensor(per_token(y[:]), per_token(y[:]),
                                         nst[:, 1, :].unsqueeze(2).to_broadcast([P, 8, C]), ALU.add))
                    link(V.tensor_tensor(y2[:], y[:], y[:], ALU.mult))
                    link(V.tensor_reduce(nst[:, 0, :], per_token(y2[:]), AX, ALU.add))
                    link(V.tensor_scalar(v, nst[:, 0, :], 1.0 / C, EPS, ALU.mult, ALU.add))
                    link(V.tensor_scalar(nsi[:], v.bitcast(I32), 1, None, ALU.logical_shift_right))
                    link(V.tensor_scalar(yy.bitcast(I32), nsi[:], -1.0, float(0x5f3759df), ALU.mult, ALU.add))
                    for _ in range(4):
                        link(V.tensor_tensor(t, yy, yy, ALU.mult))
                        link(V.tensor_tensor(t, t, v, ALU.mult))
                        link(V.tensor_scalar(t, t, -0.5, 1.5, ALU.mult, ALU.add))
                        link(V.tensor_tensor(yy, yy, t, ALU.mult))
                    assert n[0] == YCH, n
                    dve.wait_ge(out_done[o], 64 * out_before(i, s))
                    V.tensor_tensor(per_token(outb[:, o, :]), per_token(y[:]),
                                    yy.unsqueeze(2).to_broadcast([P, 8, C]), ALU.mult).then_inc(y_done, 1)

                def out_before(i, s):
                    return i - 1 if s == 0 else i
                groups(dve, step)


_INS = ['x', 'L0_tok_ln_q_w', 'L0_tok_ln_q_b', 'L0_tok_Wq', 'L0_tok_ln_kv_w', 'L0_tok_ln_kv_b', 'L0_tok_Wkv',
        'L0_tok_proj_w', 'L0_tok_proj_b', 'L0_attn_w_qkv', 'L0_attn_w_proj', 'L0_attn_b_proj', 'L0_attn_slopes',
        'L0_ffn_router_w', 'L0_ffn_w1', 'L0_ffn_b1', 'L0_ffn_w2', 'L0_ffn_b2']
_OUTS = [((128, 256, 64), 'float32')]


def kernel(**inputs):
    import numpy as _np
    import concourse.bacc as _bacc
    from concourse import mybir as _mybir
    from concourse.bass_utils import run_bass_kernel_spmd as _run

    nc = _bacc.Bacc("TRN2", target_bir_lowering=False, num_devices=1)
    arrays, args = {}, []
    for name in _INS:
        a = _np.ascontiguousarray(inputs[name])
        arrays[f"in_{name}_dram"] = a
        args.append(nc.dram_tensor(f"in_{name}_dram", a.shape, _mybir.dt.from_np(a.dtype), kind="ExternalInput").ap())
    for i, (shape, dtype) in enumerate(_OUTS):
        dt = _mybir.dt.from_np(_np.dtype(dtype))
        args.append(nc.dram_tensor(f"out_{i}_dram", shape, dt, kind="ExternalOutput").ap())
    vit_tower_kernel(nc, *args)
    r = _run(nc, [arrays], core_ids=[0])
    return r.results[0]["out_0_dram"]
```

```python
from contextlib import ExitStack

import concourse.bass as bass
from concourse import mybir

ALU = mybir.AluOpType
ACT = mybir.ActivationFunctionType
AX = mybir.AxisListType.X
F32 = mybir.dt.float32
F16 = mybir.dt.float16
I32 = mybir.dt.int32


def vit_tower_kernel(nc, x, ln_q_w, ln_q_b, Wq, ln_kv_w, ln_kv_b, Wkv, proj_w, proj_b,
                     w_qkv, w_proj, b_proj, slopes, router_w, w1, b1, w2, b2, out):
    P = 128
    B, C, HH, WW = x.shape
    ST = 4
    N = ST * ST
    PX = HH * WW // 2
    HEADS = slopes.shape[0]
    D = C // HEADS
    E = router_w.shape[0]
    SL = 2 * HEADS
    UNITS = B
    TOK_SCALE = float(C) ** -0.5
    ATT_SCALE = float(D) ** -0.5
    EPS = 1e-5
    WS = 64.0
    GN = 4
    NG = N // GN
    NS = N // 2
    assert (C, D, N, P) == (64, 8, 16, 128) and B % 2 == 0

    def done(i, s, lag, per, plus=0):
        if isinstance(i, int):
            return max(0, max(0, min(UNITS, 2 * i + s - lag + 1)) * per + plus)
        return i * (2 * per) + (s - lag + 1) * per + plus

    def there(i, s, lag):
        return not isinstance(i, int) or 0 <= 2 * i + s - lag < UNITS

    def pairs(i, back, per=1):
        if isinstance(i, int):
            return max(0, min(UNITS // 2, i + back)) * per
        return i * per + back * per

    def floor0(n):
        return max(0, n) if isinstance(n, int) else n

    def chain(eng, sem, base):
        n = [0]

        def link(ins):
            n[0] += 1
            ins.then_inc(sem, 1)
            eng.wait_ge(sem, base + n[0])
        return link, n

    def units(eng, step):
        step(-1, 1)
        for i in range(4):
            step(i, 0)
            step(i, 1)
        with eng.Fori(4, UNITS // 2 - 1) as i:
            step(i, 0)
            step(i, 1)
        for i in range(UNITS // 2 - 1, UNITS // 2 + 3):
            step(i, 0)
            step(i, 1)

    with ExitStack() as ctx:
        def sb(name, shape, dt=F32):
            return ctx.enter_context(nc.sbuf_tensor(name, shape, dt))

        def sem(name):
            return ctx.enter_context(nc.semaphore(name))

        ps = ctx.enter_context(nc.psum_tensor("ps", [P, 8, 512], F32))
        psf = ps[:].rearrange("p b c -> p (b c)")
        KB = [ps[:, 0, :], ps[:, 1, :]]
        CVB = [ps[:, 2, :], ps[:, 3, :]]
        SCB = [ps[:, 4, :], ps[:, 5, :]]
        B6 = ps[:, 6, :]
        B7 = ps[:, 7, :]

        ident = sb("ident", [P, P])
        centre2 = sb("centre2", [P, P])
        ones = sb("ones", [P, P])
        blockmask = sb("blockmask", [P, P])
        headmask = sb("headmask", [P, SL])
        w_ckv = sb("w_ckv", [P, 3 * P])
        w_h = sb("w_h", [P, 3 * P], F16)
        w_l = sb("w_l", [P, 3 * P], F16)
        w_qc = sb("w_qc", [P, 2 * P])
        w_pj = sb("w_pj", [P, P])
        w_aq = sb("w_aq", [P, P])
        w_avki = sb("w_avki", [P, 3 * P])
        w_ap = sb("w_ap", [P, P])
        bk_row = sb("bk_row", [P, P])
        bq_row = sb("bq_row", [P, P])
        bp_row = sb("bp_row", [P, P])
        bv_col = sb("bv_col", [P, 1])
        pb_col = sb("pb_col", [P, 1])
        decay = sb("decay", [P, HEADS, P])
        kdec = sb("kdec", [P, HEADS])
        qdec = sb("qdec", [P, P])
        h1 = sb("h1", [P, UNITS, P])

        with ExitStack() as early:
            def sb1(name, shape, dt=F32):
                return early.enter_context(nc.sbuf_tensor(name, shape, dt))

            sm = sb1("sm", [P, SL * P])
            cat = sm[:, 0:4 * P].rearrange("p (j c) -> p j c", j=4)
            scr = sm[:, 4 * P:8 * P].rearrange("p (j c) -> p j c", j=4)
            rows = sm[:, 8 * P:10 * P].rearrange("p (j c) -> p j c", j=4)
            lnb = sm[:, 10 * P:12 * P].rearrange("p (j c) -> p j c", j=4)
            diff = sm[:, 12 * P:13 * P]
            tril = sm[:, 13 * P:14 * P]
            qd_tok = sm[:, 14 * P:15 * P]
            col = sb1("col", [P, 8])
            diffi = sb1("diffi", [P, P], I32)
            posi = sb1("posi", [P, 1], I32)
            pos = sb1("pos", [P, 3])
            slb = sb1("slb", [P, 8])
            nsl = sb1("nsl", [P, 8])
            bprow64 = sb1("bprow64", [P, 64])
            xb = sb1("xb", [P, PX])
            xh = sb1("xh", [P, 2, PX], F16)
            xl = sb1("xl", [P, 2, PX], F16)
            xt = sb1("xt", [P, PX // 2])
            l2 = sb1("l2", [P, P])
            vs = sb1("vs", [P, 2, N * P])
            kq = sb1("kq", [P, N * P])
            pv = sb1("pv", [P, N * P])
            NV = 2 * N + 4
            ssq = sb1("ssq", [P, 2, NV])
            var = sb1("var", [P, NV])
            yrs = sb1("yrs", [P, NV])
            yt = sb1("yt", [P, NV])
            sc = sb1("sc", [P, N * SL])
            ex = sb1("ex", [P, N * SL])
            aw = sb1("aw", [P, N * SL])
            mx = sb1("mx", [P, SL])
            den = sb1("den", [P, SL])
            rden = sb1("rden", [P, SL])
            agg = sb1("agg", [P, P])
            aggn = sb1("aggn", [P, P])
            aggT = sb1("aggT", [P, P])
            red = sb1("red", [P, P])
            qps = sb1("qps", [P, P])
            hT = sb1("hT", [P, 2, P])
            qc = sb1("qc", [P, P])
            q2 = sb1("q2", [P, P])
            qq = sb1("qq", [P, 2, P])
            sbias = sb1("sbias", [P, 2, SL])
            qT = sb1("qT", [P, 2, P])
            kT = sb1("kT", [P, 2, P])
            VW = P + D
            vpad = sb1("vpad", [P, 2, SL * VW])
            vpl = sb1("vpl", [P, P])
            kpl = sb1("kpl", [P, P])
            kd = sb1("kd", [P, P])
            qdm = sb1("qdm", [P, P])
            sblk = sb1("sblk", [P, P])
            htok = sb1("htok", [P, 2, P])
            qm = sb1("qm", [P, 2, SL * P])
            oT = sb1("oT", [P, P])
            lt = sb1("lt", [P, P])

            ld_w = sem("ld_w")
            s_zero = sem("s_zero")
            s_pool0 = sem("s_pool0")
            s_set = sem("s_set")
            s_dve0 = sem("s_dve0")
            s_act0 = sem("s_act0")
            s_pe0 = sem("s_pe0")
            x_in = [sem("x_in0"), sem("x_in1")]
            hi_done = sem("hi_done")
            lo_done = sem("lo_done")
            grp = sem("grp")
            kq_done = sem("kq_done")
            cv_done = sem("cv_done")
            newt_ch = sem("newt_ch")
            dred_done = sem("dred_done")
            soft_ch = sem("soft_ch")
            s3_done = sem("s3_done")
            ex_done = sem("ex_done")
            aw_done = sem("aw_done")
            pv_done = sem("pv_done")
            agg_ch = sem("agg_ch")
            agg_done = sem("agg_done")
            agT_pe = sem("agT_pe")
            agT_ev = sem("agT_ev")
            pj_done = sem("pj_done")
            hT_done = sem("hT_done")
            xs_ch = sem("xs_ch")
            xs_done = sem("xs_done")
            rcp_done = sem("rcp_done")
            qp_pe = sem("qp_pe")
            qp_ev = sem("qp_ev")
            q_ch = sem("q_ch")
            ln_sq = sem("ln_sq")
            hb_done = sem("hb_done")
            qp_done = sem("qp_done")
            qk_pe = sem("qk_pe")
            qk_ev = sem("qk_ev")
            vk_pe = sem("vk_pe")
            vk_ev = sem("vk_ev")
            st_ev = sem("st_ev")
            kd_done = sem("kd_done")
            s_pe = sem("s_pe")
            sb_done = sem("sb_done")
            qd_done = sem("qd_done")
            qm_done = sem("qm_done")
            sc_done = sem("sc_done")
            mask_done = sem("mask_done")
            o_done = sem("o_done")
            oT_done = sem("oT_done")
            pr_done = sem("pr_done")
            lt_done = sem("lt_done")
            h1_done = sem("h1_done")

            LOADS = 24
            block = early.enter_context(nc.Block())

            xr = x.rearrange("n c (s a b) w -> (n c) s a b w", s=2, b=ST)

            def row(ap, n):
                return ap.unsqueeze(0).to_broadcast([P, n])

            @block.sync
            def _(sp):
                sp.wait_ge(s_zero, 8)
                todo = [
                    (rows[0:64, 0, :], Wq), (rows[64:128, 0, :], Wq),
                    (rows[0:64, 1, :], Wkv[0:64, :]), (rows[64:128, 1, :], Wkv[0:64, :]),
                    (rows[0:64, 2, :], Wkv[64:128, :]), (rows[64:128, 2, :], Wkv[64:128, :]),
                    (rows[0:64, 3, :], proj_w), (rows[64:128, 3, :], proj_w),
                    (lnb[:, 0, :], row(ln_q_w, 64)), (lnb[:, 1, :], row(ln_q_b, 64)),
                    (lnb[:, 2, :], row(ln_kv_w, 64)), (lnb[:, 3, :], row(ln_kv_b, 64)),
                    (bprow64[:], row(b_proj, 64)), (slb[:], row(slopes, 8)),
                ]
                for m in range(2):
                    r = slice(64 * m, 64 * m + 64)
                    todo += [
                        (pb_col[r, :], proj_b.unsqueeze(1)),
                        (w_aq[r, 64 * m:64 * m + 64], w_qkv[:, 0:64]),
                        (w_avki[r, 64 * m:64 * m + 64], w_qkv[:, 128:192]),
                        (w_avki[r, P + 64 * m:P + 64 * m + 64], w_qkv[:, 64:128]),
                        (w_ap[r, 64 * m:64 * m + 64], w_proj),
                    ]
                for dst, src in todo:
                    sp.dma_start(dst, src).then_inc(ld_w, 16)
                assert len(todo) == LOADS

                def load(i, s):
                    sp.wait_ge(lo_done, done(i, s, 1, 2))
                    for b in range(ST):
                        sp.dma_start(xb[:, b * PX // ST:(b + 1) * PX // ST].rearrange("p (a w) -> p a w", w=WW),
                                     xr[bass.ds(i * P, P), s, :, b, :]).then_inc(x_in[s], 16)
                load(0, 0)
                load(0, 1)
                with sp.Fori(1, UNITS // 2) as i:
                    load(i, 0)
                    load(i, 1)

            @block.tensor
            def _(pe):
                pe.wait_ge(s_dve0, 1)
                for j in range(4):
                    nc.tensor.transpose(ps[:, 0, j * P:(j + 1) * P], cat[:, j, :], ident[:])
                for j in range(2):
                    nc.tensor.matmul(ps[:, 1, j * P:(j + 1) * P], ones[:], scr[:, j, :], start=True, stop=True)
                pe.wait_ge(s_act0, 1)
                nc.tensor.transpose(ps[:, 1, 2 * P:3 * P], qd_tok[:], ident[:]).then_inc(s_pe0, 1)
                pe.wait_ge(s_dve0, 2)

                def step(i, s):
                    o = 1 - s
                    xhv = xh[:, s, :].rearrange("p (b k d) -> p b d k", b=ST, d=ST)
                    xlv = xl[:, s, :].rearrange("p (b k d) -> p b d k", b=ST, d=ST)

                    def two_pixels(j):
                        if not there(i, s, 0):
                            return
                        g = j // 2
                        if j == 0:
                            pe.wait_ge(lo_done, done(i, s, 0, 2))
                            pe.wait_ge(hi_done, done(i, s, 0, 2))
                        if j == 4:
                            pe.wait_ge(qp_done, done(i, s, 0, 1))
                        if j % 2 == 0:
                            pe.wait_ge(kq_done, done(i, s, 1, NG, g - 1))
                        pe.wait_ge(cv_done, done(i, s, 1, 2 * NS, 2 * (j - 1)))
                        for n in (2 * j, 2 * j + 1):
                            key = KB[g % 2][:, (n % GN) * P:(n % GN + 1) * P]
                            cv = CVB[j % 2][:, (n % 2) * 2 * P:(n % 2 + 1) * 2 * P]
                            h, l = xhv[:, n // ST, n % ST], xlv[:, n // ST, n % ST]
                            nc.tensor.matmul(key, h, w_h[:, 2 * P:3 * P], start=True, stop=False)
                            nc.tensor.matmul(key, h, w_l[:, 2 * P:3 * P], start=False, stop=False)
                            nc.tensor.matmul(key, l, w_h[:, 2 * P:3 * P], start=False, stop=True)
                            nc.tensor.matmul(cv, h, w_h[:, 0:2 * P], start=True, stop=False)
                            nc.tensor.matmul(cv[:, P:2 * P], h, w_l[:, P:2 * P], start=False, stop=False)
                            mm = nc.tensor.matmul(cv, l, w_h[:, 0:2 * P], start=False, stop=True)
                        mm.then_inc(grp, 1)

                    def queries():
                        if there(i, s, -1):
                            pe.wait_ge(xs_done, done(i, s, -1, 1))
                            pe.wait_ge(vk_ev, done(i, s, 3, 2))
                            if s == 1:
                                pe.wait_ge(st_ev, pairs(i, 0, 2))
                            nc.tensor.matmul(B6[:, 0:2 * P], red[:], w_qc[:], start=True,
                                             stop=True).then_inc(qp_pe, 1)

                    def attn_qk():
                        if there(i, s, 3):
                            pe.wait_ge(hT_done, done(i, s, 3, 1))
                            if s == 1:
                                pe.wait_ge(sb_done, pairs(i, -1))
                            nc.tensor.matmul(B6[:, 0:P], w_aq[:], hT[:, o, :], start=True, stop=True)
                            nc.tensor.matmul(B6[:, P:2 * P], w_avki[:, P:2 * P], hT[:, o, :], start=True,
                                             stop=True).then_inc(qk_pe, 1)

                    def attn_vk():
                        if there(i, s, 3):
                            pe.wait_ge(qk_ev, done(i, s, 3, 2))
                            nc.tensor.matmul(B6[:, 0:3 * P], hT[:, o, :], w_avki[:], start=True,
                                             stop=True).then_inc(vk_pe, 1)

                    def scores(r):
                        if there(i, s, 4):
                            pe.wait_ge(qm_done, done(i, s, 4, 1))
                            pe.wait_ge(qk_ev, done(i, s, 4, 2))
                            pe.wait_ge(mask_done, done(i, s, 5, 4, r - 1))
                            nc.tensor.matmul(SCB[r % 2], kT[:, s, :], qm[:, s, r * 512:(r + 1) * 512],
                                             start=True, stop=True).then_inc(sc_done, 1)

                    def attend(r):
                        if not there(i, s, 4):
                            return
                        if r == 0:
                            pe.wait_ge(lt_done, done(i, s, 5, 1))
                            pe.wait_ge(vk_ev, done(i, s, 4, 2))
                        pe.wait_ge(mask_done, done(i, s, 5, 4, r + 1))
                        for j in range(4 * r, 4 * r + 4):
                            mm = nc.tensor.matmul(B7[:, 0:P], vpad[:, s, j * P:(j + 1) * P],
                                                  sm[:, j * P:(j + 1) * P], start=(j == 0),
                                                  stop=(j == SL - 1 and s == 0))
                        if r == 3:
                            if s == 1:
                                pe.wait_ge(sb_done, pairs(i, -1))
                                pe.wait_ge(qd_done, pairs(i, -1))
                                mm = nc.tensor.matmul(B7[:, 0:P], sblk[:], qdm[:], start=False, stop=True)
                            mm.then_inc(o_done, 1)

                    def aggregated():
                        if there(i, s, 2):
                            pe.wait_ge(agg_done, done(i, s, 2, 1))
                            pe.wait_ge(qp_ev, done(i, s, -1, 1))
                            pe.wait_ge(vk_ev, done(i, s, 3, 2))
                            if s == 1:
                                pe.wait_ge(st_ev, pairs(i, 0, 2))
                            nc.tensor.transpose(B6[:, 0:P], aggn[:], ident[:]).then_inc(agT_pe, 1)

                    def projected():
                        if there(i, s, 2):
                            pe.wait_ge(agT_ev, done(i, s, 2, 1))
                            nc.tensor.matmul(B6[:, P:2 * P], w_pj[:], aggT[:], start=True,
                                             stop=True).then_inc(pj_done, 1)

                    def state():
                        if there(i, s, 4) and s == 0:
                            pe.wait_ge(kd_done, pairs(i, -1))
                            pe.wait_ge(agT_ev, done(i, s, 2, 1))
                            pe.wait_ge(hT_done, done(i, s, 2, 1))
                            pe.wait_ge(vk_ev, done(i, s, 3, 2))
                            nc.tensor.matmul(B6[:, 3 * P:4 * P], kd[:], vpl[:], start=True,
                                             stop=True).then_inc(s_pe, 1)

                    two_pixels(0)
                    scores(0)
                    attn_qk()
                    two_pixels(1)
                    scores(1)
                    two_pixels(2)
                    attn_vk()
                    attend(0)
                    queries()
                    two_pixels(3)
                    attend(1)
                    scores(2)
                    two_pixels(4)
                    aggregated()
                    scores(3)
                    two_pixels(5)
                    projected()
                    attend(2)
                    two_pixels(6)
                    attend(3)
                    two_pixels(7)
                    state()
                    if there(i, s, 4):
                        pe.wait_ge(oT_done, done(i, s, 4, 1))
                        nc.tensor.matmul(B7[:, P:2 * P], oT[:], w_ap[:], start=True, stop=True).then_inc(pr_done, 1)
                units(pe, step)

            @block.scalar
            def _(act):
                act.wait_ge(s_dve0, 1)
                for h in range(HEADS):
                    nc.scalar.activation(decay[:, h, :], diff[:], ACT.Exp, scale=nsl[:, h:h + 1])
                nc.scalar.activation(kdec[:], nsl[:], ACT.Exp, scale=pos[:, 1:2])
                nc.scalar.activation(qd_tok[:], scr[:, 2, :], ACT.Exp, scale=pos[:, 0:1]).then_inc(s_act0, 1)
                act.wait_ge(s_dve0, 2)

                def step(i, s):
                    o = 1 - s

                    def squares(src, dst, to=None):
                        return nc.scalar.activation(src if to is None else to, src, ACT.Square, accum_out=dst)

                    def pixels_values(j):
                        if not there(i, s, 0):
                            return
                        if j == 0:
                            act.wait_ge(newt_ch, (2 * i + s) * 9 + 1)
                            act.wait_ge(pv_done, done(i, s, 2, 1))
                        act.wait_ge(grp, done(i, s, 1, NS, j + 1))
                        cvw = CVB[j % 2].rearrange("p (n c) -> p n c", c=2 * P)
                        for n in range(2):
                            for m in range(2):
                                k = 4 * j + 2 * n + m
                                ins = squares(cvw[:, n, m * C:(m + 1) * C], ssq[:, s, k:k + 1])
                        ins.then_inc(cv_done, 1)
                        nc.scalar.activation(vs[:, s, 2 * j * P:(2 * j + 2) * P].rearrange("p (n c) -> p n c", c=P),
                                             cvw[:, :, P:2 * P], ACT.Copy).then_inc(cv_done, 1)

                    def high(half):
                        if there(i, s, -1):
                            act.wait_ge(x_in[o], 16 * ST * (i + 1 if s == 0 else i + 2))
                            act.wait_ge(grp, done(i, s, 1, NS))
                            at = slice(half * PX // 2, (half + 1) * PX // 2)
                            nc.scalar.activation(xh[:, o, at], xb[:, at], ACT.Copy).then_inc(hi_done, 1)

                    pixels_values(0)
                    high(0)
                    high(1)
                    if there(i, s, 3):
                        act.wait_ge(qk_pe, done(i, s, 3, 1))
                        act.wait_ge(sc_done, done(i, s, 5, 4))
                        act.wait_ge(qm_done, done(i, s, 5, 1))
                        act.wait_ge(o_done, done(i, s, 5, 1))
                        nc.scalar.activation(qT[:, o, :], B6[:, 0:P], ACT.Copy, scale=ATT_SCALE).then_inc(qk_ev, 1)
                        nc.scalar.activation(kT[:, o, :], B6[:, P:2 * P], ACT.Copy).then_inc(qk_ev, 1)
                    if there(i, s, 5):
                        act.wait_ge(lt_done, done(i, s, 5, 1))
                        for m in range(2):
                            ins = squares(lt[:, m * C:(m + 1) * C], ssq[:, o, 2 * N + m:2 * N + m + 1],
                                          l2[:, m * C:(m + 1) * C])
                        ins.then_inc(ln_sq, 1)
                    pixels_values(1)
                    if there(i, s, 3):
                        act.wait_ge(vk_pe, done(i, s, 3, 1))
                        act.wait_ge(lt_done, done(i, s, 5, 1))
                        nc.scalar.activation(
                            vpad[:, o, :].rearrange("p (j w) -> p j w", w=VW)[:, :, 0:D],
                            B6[:, 0:P].rearrange("p (j d) -> p j d", d=D), ACT.Copy).then_inc(vk_ev, 1)
                        if s == 1:
                            act.wait_ge(s_pe, pairs(i, -1))
                            act.wait_ge(kd_done, pairs(i, -1))
                            nc.scalar.activation(vpl[:], B6[:, 0:P], ACT.Copy).then_inc(st_ev, 1)
                            nc.scalar.activation(kpl[:], B6[:, P:2 * P], ACT.Copy).then_inc(st_ev, 1)
                        nc.scalar.activation(htok[:, o, :], B6[:, 2 * P:3 * P], ACT.Copy).then_inc(vk_ev, 1)
                    pixels_values(2)
                    if there(i, s, -1):
                        act.wait_ge(qp_pe, done(i, s, -1, 1))
                        act.wait_ge(qp_done, done(i, s, 0, 1))
                        nc.scalar.activation(qps[:], B6[:, 0:P], ACT.Copy)
                        for m in range(2):
                            ins = squares(B6[:, P + m * C:P + (m + 1) * C],
                                          ssq[:, o, 2 * N + 2 + m:2 * N + 3 + m])
                        ins.then_inc(qp_ev, 1)
                        nc.scalar.activation(h1[:, bass.ds(2 * i + s + 1, 1), :], red[:].unsqueeze(1),
                                             ACT.Copy, scale=1.0 / N).then_inc(rcp_done, 1)
                    pixels_values(3)
                    pixels_values(4)
                    if there(i, s, 2):
                        act.wait_ge(agT_pe, done(i, s, 2, 1))
                        act.wait_ge(pj_done, done(i, s, 3, 1))
                        nc.scalar.activation(aggT[:], B6[:, 0:P], ACT.Identity, bias=bv_col[:, 0:1],
                                             scale=1.0 / WS).then_inc(agT_ev, 1)
                    if there(i, s, 1):
                        act.wait_ge(s3_done, done(i, s, 1, 1))
                        nc.scalar.activation(ex[:], sc[:], ACT.Exp, scale=TOK_SCALE / WS).then_inc(ex_done, 1)
                    pixels_values(5)
                    pixels_values(6)
                    if there(i, s, 4):
                        act.wait_ge(o_done, done(i, s, 4, 1))
                        act.wait_ge(pr_done, done(i, s, 5, 1))
                        nc.scalar.activation(oT[:], B7[:, 0:P], ACT.Copy).then_inc(oT_done, 1)
                    pixels_values(7)
                units(act, step)

            @block.gpsimd
            def _(pool):
                for t in (w_aq, w_ap, w_avki, vpad, ident, blockmask):
                    nc.gpsimd.memset(t[:], 0.0).then_inc(s_zero, 1)
                nc.gpsimd.memset(ones[:], 1.0).then_inc(s_zero, 1)
                nc.gpsimd.memset(headmask[:], 1.0).then_inc(s_zero, 1)
                nc.gpsimd.iota(diffi[:], pattern=[[1, P]], base=0, channel_multiplier=-1).then_inc(s_pool0, 1)
                nc.gpsimd.iota(posi[:], pattern=[[0, 1]], base=0, channel_multiplier=1).then_inc(s_pool0, 1)
                link, n = chain(pool, s_pool0, 2)
                pool.wait_ge(s_pool0, 2)
                pool.wait_ge(s_zero, 8)
                link(nc.gpsimd.affine_select(out=ident[:], in_=ident[:], compare_op=ALU.not_equal, fill=1.0, base=0,
                                             pattern=[[-1, P]], channel_multiplier=1))
                for m in range(2):
                    link(nc.gpsimd.memset(blockmask[64 * m:64 * m + 64, 64 * m:64 * m + 64], 1.0))
                for base, pattern, step_p in ((0, [[-D, SL]], 1), (D - 1, [[D, SL]], -1)):
                    link(nc.gpsimd.affine_select(out=headmask[:], in_=headmask[:], compare_op=ALU.is_ge, fill=0.0,
                                                 base=base, pattern=pattern, channel_multiplier=step_p))

                def step(i, s):
                    o = 1 - s

                    if there(i, s, -1):
                        link, n = chain(pool, xs_ch, done(i, s, 0, 3))
                        pool.wait_ge(x_in[o], 16 * ST * (i + 1 if s == 0 else i + 2))
                        pool.wait_ge(xs_done, done(i, s, 0, 1))
                        link(nc.gpsimd.tensor_tensor(xt[:], xb[:, 0:PX // 2], xb[:, PX // 2:PX], ALU.add))
                        link(nc.gpsimd.tensor_tensor(xt[:, 0:PX // 4], xt[:, 0:PX // 4], xt[:, PX // 4:PX // 2],
                                                     ALU.add))
                        xp = xt[:, 0:PX // 4].rearrange("p (k d) -> p d k", d=ST)
                        link(nc.gpsimd.tensor_tensor(xp[:, 0:2, :], xp[:, 0:2, :], xp[:, 2:4, :], ALU.add))
                        pool.wait_ge(qp_pe, done(i, s, 0, 1))
                        pool.wait_ge(rcp_done, done(i, s, 0, 1))
                        nc.gpsimd.tensor_tensor(red[:], xp[:, 0, :], xp[:, 1, :], ALU.add).then_inc(xs_done, 1)
                        pool.wait_ge(hi_done, done(i, s, -1, 2))
                        at = slice(PX // 2, PX)
                        nc.gpsimd.tensor_tensor(xl[:, o, at], xb[:, at], xh[:, o, at],
                                                ALU.subtract).then_inc(lo_done, 1)
                    if there(i, s, 3):
                        pool.wait_ge(qk_ev, done(i, s, 3, 2))
                        pool.wait_ge(sc_done, done(i, s, 5, 4))
                        nc.gpsimd.tensor_tensor(
                            qm[:, o, :].rearrange("p (j c) -> p j c", c=P),
                            qT[:, o, :].unsqueeze(1).to_broadcast([P, SL, P]),
                            headmask[:].unsqueeze(2).to_broadcast([P, SL, P]), ALU.mult).then_inc(qm_done, 1)
                        pool.wait_ge(vk_ev, done(i, s, 3, 2))
                        nc.gpsimd.tensor_tensor(htok[:, o, :], htok[:, o, :], bp_row[:],
                                                ALU.add).then_inc(hb_done, 1)
                    if there(i, s, 1):
                        pool.wait_ge(aw_done, done(i, s, 1, 1))
                        pool.wait_ge(agg_done, done(i, s, 2, 1))
                        nc.gpsimd.tensor_tensor(
                            pv[:].rearrange("p (k d) -> p k d", d=D),
                            vs[:, o, :].rearrange("p (k d) -> p k d", d=D),
                            aw[:].unsqueeze(2).to_broadcast([P, N * SL, D]), ALU.mult).then_inc(pv_done, 1)
                units(pool, step)

            @block.vector
            def _(dve):
                dve.wait_ge(s_pool0, 7)
                dve.wait_ge(ld_w, 16 * LOADS)
                link, n = chain(dve, s_set, 0)
                V = nc.vector
                link(V.memset(ssq[:], 1.0))
                link(V.tensor_copy(diff[:], diffi[:]))
                link(V.tensor_scalar(tril[:], diff[:], 0.0, None, ALU.is_ge))
                link(V.tensor_scalar(diff[:], diff[:], 0.0, None, ALU.max))
                link(V.tensor_copy(pos[:, 0:1], posi[:]))
                link(V.tensor_scalar(pos[:, 1:2], pos[:, 0:1], -1.0, float(P), ALU.mult, ALU.add))
                link(V.tensor_scalar(nsl[:], slb[:], -1.0, None, ALU.mult))
                for m in range(2):
                    link(V.tensor_copy(scr[:, 2, m * C:(m + 1) * C].rearrange("p (h d) -> p h d", d=D),
                                       nsl[:].unsqueeze(2).to_broadcast([P, HEADS, D])))
                    link(V.tensor_copy(bp_row[:, m * C:(m + 1) * C], bprow64[:]))
                for j, b_at, dst in ((0, 1, col[:, 0:1]), (1, 3, col[:, 1:2]), (2, 3, bv_col[:])):
                    link(V.tensor_tensor(scr[:, 3, 0:C], rows[:, j, :], lnb[:, b_at, :], ALU.mult))
                    link(V.tensor_reduce(dst, scr[:, 3, 0:C], AX, ALU.add))
                for j, g_at in ((0, 0), (1, 2), (2, 2)):
                    link(V.tensor_tensor(rows[:, j, :], rows[:, j, :], lnb[:, g_at, :], ALU.mult))
                    link(V.tensor_reduce(col[:, 2:3], rows[:, j, :], AX, ALU.add))
                    link(V.tensor_scalar(col[:, 3:4], col[:, 2:3], -1.0 / C, None, ALU.mult))
                    link(V.tensor_scalar(rows[:, j, :], rows[:, j, :], col[:, 3:4], None, ALU.add))
                for j in range(4):
                    for m in range(2):
                        link(V.tensor_copy(cat[:, j, m * C:(m + 1) * C], rows[:, j, :]))
                link(V.tensor_scalar(scr[:, 0, :], ident[:], col[:, 0:1], None, ALU.mult))
                link(V.tensor_scalar(scr[:, 1, :], ident[:], col[:, 1:2], None, ALU.mult))
                link(V.scalar_tensor_tensor(w_ckv[:, 0:P], blockmask[:], -1.0 / C, ident[:], ALU.mult, ALU.add))
                link(V.tensor_scalar(w_qc[:, P:2 * P], w_ckv[:, 0:P], 1.0 / N, None, ALU.mult))
                link(V.tensor_copy(w_avki[:, 2 * P:3 * P], w_ckv[:, 0:P]))
                for t in (w_ap, bp_row):
                    th = t[:].rearrange("p (m c) -> p m c", c=C)
                    link(V.tensor_reduce(col[:, 4:6], th, AX, ALU.add))
                    link(V.tensor_scalar(col[:, 6:8], col[:, 4:6], -1.0 / C, None, ALU.mult))
                    link(V.tensor_tensor(th, th, col[:, 6:8].unsqueeze(2).to_broadcast([P, 2, C]), ALU.add))
                V.tensor_scalar(centre2[:], w_ckv[:, 0:P], 2.0, None, ALU.mult).then_inc(s_dve0, 1)
                dve.wait_ge(s_pe0, 1)
                for j, dst in ((0, w_qc[:, 0:P]), (1, w_ckv[:, 2 * P:3 * P]), (2, w_ckv[:, P:2 * P]), (3, w_pj[:])):
                    link(V.tensor_tensor(dst, ps[:, 0, j * P:(j + 1) * P], blockmask[:], ALU.mult))
                link(V.tensor_scalar(w_qc[:, 0:P], w_qc[:, 0:P], 1.0 / N, None, ALU.mult))
                link(V.tensor_copy(bq_row[:], ps[:, 1, 0:P]))
                link(V.tensor_scalar(bk_row[:], ps[:, 1, P:2 * P], WS, None, ALU.mult))
                link(V.tensor_scalar(w_ckv[:, P:3 * P], w_ckv[:, P:3 * P], WS, None, ALU.mult))
                link(V.tensor_copy(w_h[:], w_ckv[:]))
                link(V.tensor_tensor(w_l[:], w_ckv[:], w_h[:], ALU.subtract))
                link(V.tensor_copy(qdec[:], ps[:, 1, 2 * P:3 * P]))
                V.tensor_tensor(decay[:], decay[:], tril[:].unsqueeze(1).to_broadcast([P, HEADS, P]),
                                ALU.mult).then_inc(s_dve0, 1)
                dve.wait_ge(s_dve0, 2)

                def heads(ap):
                    return ap.rearrange("p (m c) -> p m c", c=C)

                def step(i, s):
                    o = 1 - s

                    def keys(g):
                        if there(i, s, 0):
                            dve.wait_ge(grp, done(i, s, 1, NS, 2 * g + 2))
                            V.tensor_tensor(kq[:, g * GN * P:(g + 1) * GN * P].rearrange("p (n c) -> p n c", c=P),
                                            KB[g % 2].rearrange("p (n c) -> p n c", c=P),
                                            qq[:, s, :].unsqueeze(1).to_broadcast([P, GN, P]),
                                            ALU.mult).then_inc(kq_done, 1)

                    def mask(r):
                        if there(i, s, 4):
                            if r == 0:
                                dve.wait_ge(o_done, done(i, s, 5, 1))
                            dve.wait_ge(sc_done, done(i, s, 5, 4, r + 1))
                            V.tensor_tensor(sm[:, r * 512:(r + 1) * 512].rearrange("p (h c) -> p h c", c=P),
                                            SCB[r % 2].rearrange("p (h c) -> p h c", c=P),
                                            decay[:, 4 * (r % 2):4 * (r % 2) + 4, :], ALU.mult).then_inc(mask_done, 1)

                    if there(i, s, 4) and s == 1:
                        dve.wait_ge(o_done, done(i, s, 6, 1))
                        V.tensor_tensor(qdm[:], qT[:, s, :], qdec[:], ALU.mult).then_inc(qd_done, 1)
                    if there(i, s, 1):
                        dve.wait_ge(kq_done, done(i, s, 1, NG))
                        V.tensor_reduce(sc[:], kq[:].rearrange("p (k d) -> p k d", d=D), AX,
                                        ALU.add).then_inc(dred_done, 1)
                    mask(0)
                    if there(i, s, 2):
                        dve.wait_ge(pv_done, done(i, s, 2, 1))
                        V.tensor_reduce(agg[:], pv[:].rearrange("p (n c) -> p c n", c=P), AX,
                                        ALU.add).then_inc(agg_ch, 1)
                    mask(1)
                    if there(i, s, -1):
                        dve.wait_ge(hi_done, done(i, s, -1, 2, -1))
                        at = slice(0, PX // 2)
                        V.tensor_tensor(xl[:, o, at], xb[:, at], xh[:, o, at],
                                        ALU.subtract).then_inc(lo_done, 1)
                    if there(i, s, 2):
                        dve.wait_ge(agg_ch, done(i, s, 2, 1))
                        dve.wait_ge(agT_pe, done(i, s, 3, 1))
                        V.tensor_tensor(aggn[:].rearrange("p (j d) -> p j d", d=D),
                                        agg[:].rearrange("p (j d) -> p j d", d=D),
                                        rden[:].unsqueeze(2).to_broadcast([P, SL, D]), ALU.mult).then_inc(agg_done, 1)
                    if there(i, s, 0):
                        dve.wait_ge(dred_done, done(i, s, 1, 1))
                    keys(0)
                    link, n = chain(dve, newt_ch, (2 * i + s + 1) * 9)
                    dve.wait_ge(cv_done, done(i, s, 1, 2 * NS))
                    dve.wait_ge(qp_ev, done(i, s, -1, 1))
                    dve.wait_ge(ln_sq, done(i, s, 5, 1))
                    link(V.tensor_scalar(var[:], ssq[:, o, :], 64.0 / 9.0 / C, 64.0 / 9.0 * EPS, ALU.mult, ALU.add))
                    link(V.tensor_scalar(yrs[:].bitcast(I32), var[:].bitcast(I32), -0.5, float(0x5f3759df),
                                         ALU.mult, ALU.add))
                    link(V.tensor_tensor(yt[:], yrs[:], yrs[:], ALU.mult))
                    link(V.tensor_tensor(yt[:], yt[:], var[:], ALU.mult))
                    link(V.scalar_tensor_tensor(yt[:], yt[:], -10.0 / 3.0, yt[:], ALU.add, ALU.mult))
                    link(V.scalar_tensor_tensor(yrs[:], yt[:], 5.0, yrs[:], ALU.add, ALU.mult))
                    link(V.scalar_tensor_tensor(yt[:], yrs[:], -9.0 / 128.0, yrs[:], ALU.mult, ALU.mult))
                    link(V.tensor_tensor(yt[:], yt[:], var[:], ALU.mult))
                    link(V.scalar_tensor_tensor(yrs[:], yt[:], 1.5, yrs[:], ALU.add, ALU.mult))
                    assert n[0] == 9
                    rs_b = yrs[:, 0:2 * N].unsqueeze(2).to_broadcast([P, 2 * N, HEADS])
                    link_q, nq = chain(dve, q_ch, done(i, s, 0, 3))
                    link, n = chain(dve, soft_ch, done(i, s, 2, 5))
                    if there(i, s, 1):
                        dve.wait_ge(dred_done, done(i, s, 1, 1))
                        dve.wait_ge(qp_done, done(i, s, 1, 1))
                        s3 = sc[:].rearrange("p (k h) -> p k h", h=HEADS)
                        sn = sc[:].rearrange("p (n j) -> p n j", j=SL)
                        link(V.tensor_tensor(s3, s3, rs_b, ALU.mult))
                        link(V.tensor_tensor(sn, sn, sbias[:, o, :].unsqueeze(1).to_broadcast([P, N, SL]), ALU.add))
                        link(V.tensor_reduce(mx[:], sc[:].rearrange("p (n j) -> p j n", j=SL), AX, ALU.max))
                        V.tensor_tensor(sn, sn, mx[:].unsqueeze(1).to_broadcast([P, N, SL]),
                                        ALU.subtract).then_inc(s3_done, 1)
                    mask(2)
                    keys(1)
                    mask(3)
                    if there(i, s, 3) and s == 1:
                        dve.wait_ge(st_ev, pairs(i, 0, 2))
                        dve.wait_ge(s_pe, pairs(i, -1))
                        V.tensor_tensor(kd[:].rearrange("p (m h d) -> p m h d", m=2, d=D),
                                        kpl[:].rearrange("p (m h d) -> p m h d", m=2, d=D),
                                        kdec[:].unsqueeze(1).unsqueeze(3).to_broadcast([P, 2, HEADS, D]),
                                        ALU.mult).then_inc(kd_done, 1)
                    if there(i, s, 5):
                        V.tensor_tensor(h1[:, bass.ds(2 * i + s - 5, 1), :].rearrange("p u (m c) -> p (u m) c", c=C),
                                        heads(lt[:]), yrs[:, 2 * N:2 * N + 2].unsqueeze(2).to_broadcast([P, 2, C]),
                                        ALU.mult).then_inc(h1_done, 1)
                    if there(i, s, -1):
                        link_q(V.tensor_tensor(heads(q2[:]), heads(qps[:]),
                                               yrs[:, 2 * N + 2:2 * N + 4].unsqueeze(2).to_broadcast([P, 2, C]),
                                               ALU.mult))
                    if there(i, s, 1):
                        dve.wait_ge(ex_done, done(i, s, 1, 1))
                        V.tensor_tensor(aw[:].rearrange("p (k h) -> p k h", h=HEADS),
                                        ex[:].rearrange("p (k h) -> p k h", h=HEADS), rs_b,
                                        ALU.mult).then_inc(aw_done, 1)
                        link(V.tensor_reduce(den[:], ex[:].rearrange("p (n j) -> p j n", j=SL), AX, ALU.add))
                    if there(i, s, -1):
                        link_q(V.tensor_tensor(qq[:, o, :], q2[:], bq_row[:], ALU.add))
                        link_q(V.tensor_tensor(qc[:], qq[:, o, :], bk_row[:], ALU.mult))
                        assert nq[0] == 3
                        V.tensor_reduce(sbias[:, o, :], qc[:].rearrange("p (j d) -> p j d", d=D), AX,
                                        ALU.add).then_inc(qp_done, 1)
                    if there(i, s, 1):
                        link(V.reciprocal(rden[:], den[:]))
                        assert n[0] == 5
                    if there(i, s, 2):
                        dve.wait_ge(pj_done, done(i, s, 2, 1))
                        dve.wait_ge(vk_pe, done(i, s, 4, 1))
                        dve.wait_ge(rcp_done, done(i, s, 2, 1))
                        V.scalar_tensor_tensor(hT[:, s, :].unsqueeze(1), B6[:, P:2 * P].unsqueeze(1), pb_col[:, 0:1],
                                               h1[:, bass.ds(2 * i + s - 2, 1), :],
                                               ALU.add, ALU.add).then_inc(hT_done, 1)
                    keys(2)
                    keys(3)
                    if there(i, s, 4) and s == 0:
                        dve.wait_ge(s_pe, pairs(i, -1))
                        dve.wait_ge(o_done, done(i, s, 5, 1))
                        V.tensor_tensor(sblk[:].rearrange("p (j d) -> p j d", d=D),
                                        B6[:, 3 * P:4 * P].rearrange("p (j d) -> p j d", d=D),
                                        headmask[:].unsqueeze(2).to_broadcast([P, SL, D]),
                                        ALU.mult).then_inc(sb_done, 1)
                    if there(i, s, 4):
                        dve.wait_ge(pr_done, done(i, s, 4, 1))
                        dve.wait_ge(h1_done, done(i, s, 5, 1))
                        dve.wait_ge(hb_done, done(i, s, 4, 1))
                        V.tensor_tensor(lt[:], B7[:, P:2 * P], htok[:, s, :], ALU.add).then_inc(lt_done, 1)
                units(dve, step)

        G = UNITS // 4
        with ExitStack() as late:
            def sb2(name, shape, dt=F32):
                return late.enter_context(nc.sbuf_tensor(name, shape, dt))

            w1bd = sb2("w1bd", [P, E, P])
            w2bd = sb2("w2bd", [P, E, P])
            rt = sb2("rt", [P, 2 * E])
            b1c = sb2("b1c", [P, E])
            b2v = sb2("b2v", [P, 4, P])
            lg = sb2("lg", [P, 2 * UNITS, E])
            ra = sb2("ra", [P, 2 * UNITS, E])
            rb = sb2("rb", [P, 2 * UNITS, E])
            comb = sb2("comb", [P, 2 * UNITS, E])
            r1 = sb2("r1", [P, 2 * UNITS])
            r2 = sb2("r2", [P, 2 * UNITS])
            rank = sb2("rank", [P, E])
            st = sb2("st", [P, 2, 4 * P])
            tokT = sb2("tokT", [P, 2, 4 * P])
            cb = sb2("cb", [P, 2, P])
            cbT = sb2("cbT", [P, 2, P])
            hid = sb2("hid", [P, 2, E, 4 * P])
            pr = sb2("pr", [P, E, P])
            y = sb2("y", [P, 4 * P])
            y2 = sb2("y2", [P, 4 * P])
            nst = sb2("nst", [P, 8, 8])
            outb = sb2("outb", [P, 2, 4 * P])

            ld2 = sem("ld2")
            z2 = sem("z2")
            st_a = sem("st_a")
            tr_a = sem("tr_a")
            tv_a = sem("tv_a")
            lg_pe = sem("lg_pe")
            lg_done = sem("lg_done")
            rt_ch = sem("rt_ch")
            rt_sub = sem("rt_sub")
            rt_exp = sem("rt_exp")
            comb_done = sem("comb_done")
            st_b = sem("st_b")
            tr_b = sem("tr_b")
            tv_b = sem("tv_b")
            up_done = sem("up_done")
            gelu_done = sem("gelu_done")
            dn_done = sem("dn_done")
            x0_done = sem("x0_done")
            pr_read = sem("pr_read")
            x0_read = sem("x0_read")
            y_ch = sem("y_ch")
            y_done = sem("y_done")
            out_done = [sem("out_done0"), sem("out_done1")]

            def gdone(i, s, lag, per):
                if isinstance(i, int):
                    return max(0, min(G, 2 * i + s - lag + 1)) * per
                return i * (2 * per) + (s - lag + 1) * per

            def gthere(i, s, lag):
                return not isinstance(i, int) or 0 <= 2 * i + s - lag < G

            def groups(eng, step):
                for i in (0, 1):
                    step(i, 0)
                    step(i, 1)
                with eng.Fori(2, G // 2 - 1) as i:
                    step(i, 0)
                    step(i, 1)
                step(G // 2 - 1, 0)
                step(G // 2 - 1, 1)
                step(G // 2, 0)

            block2 = late.enter_context(nc.Block())
            LOADS2 = 16

            @block2.gpsimd
            def _(pool):
                for t in (w1bd, w2bd, rt, b2v, cb):
                    nc.gpsimd.memset(t[:], 0.0).then_inc(z2, 1)
                for e in range(E):
                    nc.gpsimd.memset(rank[:, e:e + 1], float(E - e)).then_inc(z2, 1)

            @block2.sync
            def _(sp):
                sp.wait_ge(z2, 5 + E)
                todo = []
                for m in range(2):
                    r = slice(64 * m, 64 * m + 64)
                    todo += [(w1bd[r, :, r], w1.rearrange("e i o -> i e o")),
                             (w2bd[r, :, r], w2.rearrange("e i o -> i e o")),
                             (rt[r, m * E:(m + 1) * E], router_w.rearrange("e c -> c e")),
                             (b1c[r, :], b1.rearrange("e c -> c e"))]
                    todo += [(b2v[k * 2 * E + m * E:k * 2 * E + (m + 1) * E, k, r], b2) for k in range(4)]
                assert len(todo) == LOADS2
                for dst, src in todo:
                    sp.dma_start(dst, src, allow_slow_non_contiguous=True).then_inc(ld2, 16)

                def store(i, s):
                    sp.wait_ge(y_done, gdone(i, s, 0, 1))
                    for a in range(2):
                        for c in range(2):
                            k = 2 * a + c
                            sp.dma_start(out[bass.ds(i * 8 + 4 * s + 2 * a, 2), c * P:(c + 1) * P, :].rearrange(
                                "m p d -> p m d"), outb[:, s, k * P:(k + 1) * P].rearrange(
                                "p (m d) -> p m d", m=2)).then_inc(out_done[s], 16)
                with sp.Fori(0, G // 2) as i:
                    store(i, 0)
                    store(i, 1)
                for s in range(2):
                    sp.wait_ge(out_done[s], G // 2 * 64)

            @block2.tensor
            def _(pe):
                pe.wait_ge(ld2, 16 * LOADS2)

                def logits(i, s):
                    o = 1 - s
                    if gthere(i, s, 0):
                        pe.wait_ge(st_a, gdone(i, s, 0, 1))
                        pe.wait_ge(tv_a, gdone(i, s, 2, 1))
                        for k in range(4):
                            mm = nc.tensor.transpose(ps[:, s, k * P:(k + 1) * P], st[:, s, k * P:(k + 1) * P],
                                                     ident[:])
                        mm.then_inc(tr_a, 1)
                    if gthere(i, s, 1):
                        pe.wait_ge(tv_a, gdone(i, s, 1, 1))
                        pe.wait_ge(lg_done, gdone(i, s, 3, 1))
                        for k in range(4):
                            mm = nc.tensor.matmul(ps[:, 2 + o, k * 2 * E:(k + 1) * 2 * E],
                                                  tokT[:, o, k * P:(k + 1) * P], rt[:], start=True, stop=True)
                        mm.then_inc(lg_pe, 1)
                groups(pe, logits)

                def turn(i, s):
                    pe.wait_ge(st_b, gdone(i, s, 0, 2))
                    pe.wait_ge(tv_b, gdone(i, s, 1, 2))
                    for k in range(4):
                        nc.tensor.transpose(ps[:, 0, k * P:(k + 1) * P], st[:, s, k * P:(k + 1) * P], ident[:])
                    nc.tensor.transpose(ps[:, 1, 0:P], cb[:, s, :], ident[:]).then_inc(tr_b, 1)

                def step(i, s):
                    o = 1 - s
                    if isinstance(i, int) and i == 0 and s == 0:
                        turn(i, s)
                    for e in range(E):
                        if e == E - 1 and gthere(i, s, -1):
                            if s == 0:
                                turn(i, 1)
                            else:
                                turn(i + 1, 0)
                        if gthere(i, s, 0):
                            if e == 0:
                                pe.wait_ge(tv_b, gdone(i, s, 0, 2))
                            pe.wait_ge(gelu_done, floor0(gdone(i, s, 1, E) + e - 1))
                            nc.tensor.matmul(ps[:, 2 + e % 2, :], w1bd[:, e, :], tokT[:, s, :], start=True,
                                             stop=True).then_inc(up_done, 1)
                        if gthere(i, s, 1):
                            k, f = e // 2, e % 2
                            if e == 0:
                                pe.wait_ge(gelu_done, gdone(i, s, 1, E))
                            pe.wait_ge(pr_read, floor0(gdone(i, s, 2, 8) + e - 1))
                            for q in range(4):
                                mm = nc.tensor.matmul(ps[:, 4 + f, q * P:(q + 1) * P],
                                                      hid[:, o, 4 * f + q, k * P:(k + 1) * P],
                                                      w2bd[:, 4 * f + q, :], start=True, stop=True)
                            mm.then_inc(dn_done, 1)
                            if f == 1:
                                pe.wait_ge(x0_read, floor0(gdone(i, s, 2, 4) + k - 1))
                                nc.tensor.matmul(ps[:, 6 + k % 2, 0:P], cbT[:, o, :], b2v[:, k, :],
                                                 start=True, stop=False)
                                nc.tensor.matmul(ps[:, 6 + k % 2, 0:P], tokT[:, o, k * P:(k + 1) * P], centre2[:],
                                                 start=False, stop=True).then_inc(x0_done, 1)
                pe.wait_ge(rt_ch, 6)
                groups(pe, step)

            @block2.scalar
            def _(act):
                act.wait_ge(z2, 5 + E)

                def logits(i, s):
                    o = 1 - s
                    if gthere(i, s, -1):
                        act.wait_ge(tr_a, gdone(i, s, 1, 1))
                        nc.scalar.activation(st[:, o, :].rearrange("p (k c) -> p k c", c=P),
                                             h1[:, bass.ds(i * 8 + 4 * s + 4, 4), :], ACT.Copy).then_inc(st_a, 1)
                    if gthere(i, s, 0):
                        act.wait_ge(tr_a, gdone(i, s, 0, 1))
                        act.wait_ge(lg_pe, gdone(i, s, 2, 1))
                        nc.scalar.activation(tokT[:, s, :], ps[:, s, :], ACT.Copy).then_inc(tv_a, 1)
                    if gthere(i, s, 1):
                        act.wait_ge(lg_pe, gdone(i, s, 1, 1))
                        nc.scalar.activation(lg[:, bass.ds(i * 16 + 8 * s - 8, 8), :],
                                             ps[:, 2 + o, 0:8 * E].rearrange("p (t e) -> p t e", e=E),
                                             ACT.Copy).then_inc(lg_done, 1)
                nc.scalar.activation(st[:, 0, :].rearrange("p (k c) -> p k c", c=P), h1[:, 0:4, :],
                                     ACT.Copy).then_inc(st_a, 1)
                groups(act, logits)
                act.wait_ge(rt_sub, 1)
                nc.scalar.activation(lg[:], lg[:], ACT.Exp).then_inc(rt_exp, 1)

                def stage(i, s):
                    act.wait_ge(tr_b, gdone(i, s, 2, 1))
                    nc.scalar.activation(st[:, s, :].rearrange("p (k c) -> p k c", c=P),
                                         h1[:, bass.ds(i * 8 + 4 * s, 4), :], ACT.Copy).then_inc(st_b, 1)
                    nc.scalar.activation(cb[:, s, 0:8 * E].rearrange("p (t e) -> p t e", e=E),
                                         comb[:, bass.ds(i * 16 + 8 * s, 8), :], ACT.Copy).then_inc(st_b, 1)

                act.wait_ge(comb_done, 1)
                stage(0, 0)

                def step(i, s):
                    if gthere(i, s, 0):
                        act.wait_ge(tr_b, gdone(i, s, 0, 1))
                        act.wait_ge(x0_done, gdone(i, s, 2, 4))
                        nc.scalar.activation(tokT[:, s, :], ps[:, 0, :], ACT.Copy).then_inc(tv_b, 1)
                        nc.scalar.activation(cbT[:, s, :], ps[:, 1, 0:P], ACT.Copy).then_inc(tv_b, 1)
                        act.wait_ge(dn_done, gdone(i, s, 2, 8))
                        for e in range(E):
                            if e == E // 2 and gthere(i, s, -1):
                                if s == 0:
                                    stage(i, 1)
                                else:
                                    stage(i + 1, 0)
                            act.wait_ge(up_done, floor0(gdone(i, s, 0, E) - E + 1 + e))
                            nc.scalar.activation(hid[:, s, e, :], ps[:, 2 + e % 2, :], ACT.Gelu,
                                                 bias=b1c[:, e:e + 1]).then_inc(gelu_done, 1)
                groups(act, step)

            @block2.vector
            def _(dve):
                V = nc.vector
                dve.wait_ge(z2, 5 + E)
                dve.wait_ge(ld2, 16 * LOADS2)
                T = 2 * UNITS
                link, n = chain(dve, rt_ch, 0)
                for t, w in ((w2bd, 2 * E), (b2v, 2 * 4)):
                    th = t[:].rearrange("p e (m c) -> p (e m) c", c=C)
                    link(V.tensor_reduce(r1[:, 0:w], th, AX, ALU.add))
                    link(V.tensor_scalar(r2[:, 0:w], r1[:, 0:w], -1.0 / C, None, ALU.mult))
                    link(V.tensor_tensor(th, th, r2[:, 0:w].unsqueeze(2).to_broadcast([P, w, C]), ALU.add))
                dve.wait_ge(lg_done, G)

                def over_e(ap):
                    return ap.unsqueeze(2).to_broadcast([P, T, E])

                rank_b = rank[:].unsqueeze(1).to_broadcast([P, T, E])
                link(V.tensor_reduce(r1[:], lg[:], AX, ALU.max))
                V.tensor_tensor(lg[:], lg[:], over_e(r1[:]), ALU.subtract).then_inc(rt_sub, 1)
                dve.wait_ge(rt_exp, 1)
                link(V.tensor_reduce(r1[:], lg[:], AX, ALU.add))
                link(V.reciprocal(r2[:], r1[:]))
                link(V.tensor_tensor(lg[:], lg[:], over_e(r2[:]), ALU.mult))

                def first_largest(src, hot):
                    link(V.tensor_reduce(r1[:], src, AX, ALU.max))
                    link(V.tensor_tensor(hot, src, over_e(r1[:]), ALU.is_equal))
                    link(V.tensor_tensor(hot, hot, rank_b, ALU.mult))
                    link(V.tensor_reduce(r2[:], hot, AX, ALU.max))
                    link(V.tensor_tensor(hot, hot, over_e(r2[:]), ALU.is_equal))
                first_largest(lg[:], ra[:])
                link(V.scalar_tensor_tensor(comb[:], ra[:], -2.0, lg[:], ALU.mult, ALU.add))
                first_largest(comb[:], rb[:])
                link(V.tensor_tensor(ra[:], ra[:], rb[:], ALU.add))
                link(V.tensor_tensor(lg[:], lg[:], ra[:], ALU.mult))
                link(V.tensor_reduce(r1[:], lg[:], AX, ALU.add))
                link(V.tensor_scalar(r1[:], r1[:], 1e-12, None, ALU.max))
                link(V.reciprocal(r2[:], r1[:]))
                V.tensor_tensor(comb[:], lg[:], over_e(r2[:]), ALU.mult).then_inc(comb_done, 1)

                def per_token(ap):
                    return ap.rearrange("p (t c) -> p t c", c=C)

                def step(i, s):
                    o = 1 - s
                    if not gthere(i, s, 1):
                        return
                    YCH = 4 + 2 + 9
                    link, n = chain(dve, y_ch, gdone(i, s, 2, YCH))
                    if isinstance(i, int) and i == 0:
                        dve.wait_ge(comb_done, 1)
                    for k in range(4):
                        for f in range(2):
                            j = 2 * k + f
                            dve.wait_ge(dn_done, floor0(gdone(i, s, 1, 8) - 7 + j))
                            wv = comb[:, bass.ds(i * 16 + 8 * s - 8 + 2 * k, 2), 4 * f:4 * f + 4].rearrange(
                                "p m e -> p e m")
                            ins = V.tensor_tensor(
                                pr[:, 4 * f:4 * f + 4, :].rearrange("p e (m c) -> p e m c", c=C),
                                ps[:, 4 + f, :].rearrange("p (e m c) -> p e m c", e=4, c=C),
                                wv.unsqueeze(3).to_broadcast([P, 4, 2, C]), ALU.mult)
                            ins.then_inc(pr_read, 1)
                        dve.wait_ge(pr_read, floor0(gdone(i, s, 1, 8) - 6 + 2 * k))
                        link(V.tensor_reduce(y[:, k * P:(k + 1) * P], pr[:].rearrange("p e c -> p c e"), AX, ALU.add))
                        dve.wait_ge(x0_done, floor0(gdone(i, s, 1, 4) - 3 + k))
                        ins = V.tensor_tensor(y[:, k * P:(k + 1) * P], ps[:, 6 + k % 2, 0:P],
                                              y[:, k * P:(k + 1) * P], ALU.add)
                        ins.then_inc(x0_read, 1)
                        dve.wait_ge(x0_read, floor0(gdone(i, s, 1, 4) - 3 + k))
                    v, t, yy = nst[:, 2, :], nst[:, 3, :], nst[:, 4, :]
                    link(V.tensor_tensor(y2[:], y[:], y[:], ALU.mult))
                    link(V.tensor_reduce(nst[:, 0, :], per_token(y2[:]), AX, ALU.add))
                    link(V.tensor_scalar(v, nst[:, 0, :], 64.0 / 9.0 / C, 64.0 / 9.0 * EPS, ALU.mult, ALU.add))
                    link(V.tensor_scalar(yy.bitcast(I32), v.bitcast(I32), -0.5, float(0x5f3759df), ALU.mult, ALU.add))
                    link(V.tensor_tensor(t, yy, yy, ALU.mult))
                    link(V.tensor_tensor(t, t, v, ALU.mult))
                    link(V.scalar_tensor_tensor(t, t, -10.0 / 3.0, t, ALU.add, ALU.mult))
                    link(V.scalar_tensor_tensor(yy, t, 5.0, yy, ALU.add, ALU.mult))
                    link(V.scalar_tensor_tensor(t, yy, -9.0 / 128.0, yy, ALU.mult, ALU.mult))
                    link(V.tensor_tensor(t, t, v, ALU.mult))
                    link(V.scalar_tensor_tensor(yy, t, 1.5, yy, ALU.add, ALU.mult))
                    assert n[0] == YCH, n
                    dve.wait_ge(out_done[o], 64 * out_before(i, s))
                    V.tensor_tensor(per_token(outb[:, o, :]), per_token(y[:]),
                                    yy.unsqueeze(2).to_broadcast([P, 8, C]), ALU.mult).then_inc(y_done, 1)

                def out_before(i, s):
                    return i - 1 if s == 0 else i
                groups(dve, step)


_INS = ['x', 'L0_tok_ln_q_w', 'L0_tok_ln_q_b', 'L0_tok_Wq', 'L0_tok_ln_kv_w', 'L0_tok_ln_kv_b', 'L0_tok_Wkv',
        'L0_tok_proj_w', 'L0_tok_proj_b', 'L0_attn_w_qkv', 'L0_attn_w_proj', 'L0_attn_b_proj', 'L0_attn_slopes',
        'L0_ffn_router_w', 'L0_ffn_w1', 'L0_ffn_b1', 'L0_ffn_w2', 'L0_ffn_b2']
_OUTS = [((128, 256, 64), 'float32')]


def kernel(**inputs):
    import numpy as _np
    import concourse.bacc as _bacc
    from concourse import mybir as _mybir
    from concourse.bass_utils import run_bass_kernel_spmd as _run

    nc = _bacc.Bacc("TRN2", target_bir_lowering=False, num_devices=1)
    arrays, args = {}, []
    for name in _INS:
        a = _np.ascontiguousarray(inputs[name])
        arrays[f"in_{name}_dram"] = a
        args.append(nc.dram_tensor(f"in_{name}_dram", a.shape, _mybir.dt.from_np(a.dtype), kind="ExternalInput").ap())
    for i, (shape, dtype) in enumerate(_OUTS):
        dt = _mybir.dt.from_np(_np.dtype(dtype))
        args.append(nc.dram_tensor(f"out_{i}_dram", shape, dt, kind="ExternalOutput").ap())
    vit_tower_kernel(nc, *args)
    r = _run(nc, [arrays], core_ids=[0])
    return r.results[0]["out_0_dram"]
```
